# Optimizing a Trainium2 kernel written in Bass

```python
import numpy as np
import jax
import jax.numpy as jnp

def _softmax(x, axis=-1):
    return jax.nn.softmax(x, axis=axis)

def _gelu(x):
    return jax.nn.gelu(x, approximate=True)

def _silu(x):
    return jax.nn.silu(x)

def _sigmoid(x):
    return jax.nn.sigmoid(x)

def _layernorm(x, axis=-1, eps=1e-05):
    m = jnp.mean(x, axis=axis, keepdims=True)
    v = jnp.var(x, axis=axis, keepdims=True)
    return (x - m) / jnp.sqrt(v + eps)

def _scatter_add(tgt, idx, src, axis=0):
    return tgt.at[idx].add(src)

def _segment_sum(src, seg, n):
    return jax.ops.segment_sum(src, seg, n)
kernel_name = 'mk_adaln_ffn_d2_seqx_r4_884cfa'

def setup_inputs(seed: int=0):
    np.random.seed(seed)
    _w = jnp.asarray

    def _rec_inputs():
        import jax
        import jax.numpy as jnp
        _rk = jax.random.key(seed)
        x = -0.000125 + 0.9999 * jax.random.normal(jax.random.fold_in(_rk, 1), (8, 512, 256), jnp.float32)
        _lenS = 512 - jax.random.randint(jax.random.fold_in(_rk, 7), (8,), 0, max(1, 512 // 4) + 1, jnp.int32)
        _lenS2 = 512 - jax.random.randint(jax.random.fold_in(_rk, 8), (8,), 0, max(1, 512 // 4) + 1, jnp.int32)
        cond_256 = -0.0209273 + 1.04763 * jax.random.normal(jax.random.fold_in(_rk, 11), (8, 64), jnp.float32)
        cond_64 = 0.0223021 + 1.01123 * jax.random.normal(jax.random.fold_in(_rk, 12), (8, 64), jnp.float32)
        return (x, cond_256, cond_64)
    x, cond_256, cond_64 = _rec_inputs()

    def _L0_cond_setup():
        import math
        import jax, jax.numpy as jnp
        import numpy as np
        from jax.scipy.linalg import cholesky, solve_triangular
        B, S, D, O, K, R = (4, 2048, 256, 256, 64, 64)

        def build_dct_basis(dim: int, num_bases: int) -> np.ndarray:
            num_bases = min(num_bases, dim)
            positions = np.arange(dim, dtype=np.float32)[None, :]
            modes = np.arange(num_bases, dtype=np.float32)[:, None]
            basis = np.cos(math.pi / float(dim) * (positions + 0.5) * modes)
            basis[0] = basis[0] / math.sqrt(2.0)
            basis = basis * math.sqrt(2.0 / float(dim))
            return basis.astype(np.float32)

        def _orthogonalize_mode_to_rank(raw: jnp.ndarray) -> jnp.ndarray:
            raw = raw.astype(jnp.float32)
            gram = raw.T @ raw
            eye = jnp.eye(raw.shape[1], dtype=jnp.float32)
            chol = cholesky(gram + 0.0001 * eye, lower=True)
            inv_chol = solve_triangular(chol, eye, lower=True)
            q = raw @ inv_chol.T
            signs = jnp.sign(jnp.sum(q * raw, axis=0, keepdims=True))
            signs = jnp.where(signs == 0, jnp.ones_like(signs), signs)
            return q * signs
        key = jax.random.key(seed)
        k1, k2, k3, k4, k5 = jax.random.split(key, 5)
        x = jax.random.normal(k1, (B, S, D), dtype=jnp.float32)
        spectral_coeff = jax.random.normal(k2, (B, K), dtype=jnp.float32)
        rank_coeff = jax.random.normal(k3, (B, R), dtype=jnp.float32)
        input_basis = jnp.asarray(build_dct_basis(D, K))
        diag = min(K, R)
        mode_to_rank = 0.02 * jax.random.normal(k4, (K, R), dtype=jnp.float32)
        mode_to_rank = mode_to_rank.at[:diag, :diag].add(jnp.eye(diag, dtype=jnp.float32))
        output_basis = 0.02 * jax.random.normal(k5, (R, O), dtype=jnp.float32)
        return {'x': x, 'spectral_coeff': spectral_coeff, 'rank_coeff': rank_coeff, 'input_basis': input_basis, 'mode_to_rank': mode_to_rank, 'output_basis': output_basis}
    _L0_cond_all = _L0_cond_setup()
    _L0_cond_in = {k: v for k, v in _L0_cond_all.items() if k in ('input_basis', 'mode_to_rank', 'output_basis')}
    del _L0_cond_all

    def _L0_ffn_setup():
        import jax, jax.numpy as jnp
        import numpy as np
        EPS = 1e-09
        key = jax.random.key(seed)
        k0, k1, k2, k3 = jax.random.split(key, 4)
        B, S, H, F, E = (4, 512, 256, 512, 8)
        return {'hidden_states': jax.random.normal(k0, (B, S, H), dtype=jnp.float32), 'router_w': jax.random.normal(k1, (H, E), dtype=jnp.float32) * 0.02, 'w1': jax.random.normal(k2, (E, H, F), dtype=jnp.float32) * 0.02, 'w2': jax.random.normal(k3, (E, F, H), dtype=jnp.float32) * 0.02}
    _L0_ffn_all = _L0_ffn_setup()
    _L0_ffn_in = {k: v for k, v in _L0_ffn_all.items() if k in ('router_w', 'w1', 'w2')}
    del _L0_ffn_all

    def _L1_cond_setup():
        import jax, jax.numpy as jnp
        import numpy as np
        EPS = 1e-08

        def hamilton(q1, q2):
            w1, x1, y1, z1 = (q1[..., i, :] for i in range(4))
            w2, x2, y2, z2 = (q2[..., i, :] for i in range(4))
            w = w1 * w2 - x1 * x2 - y1 * y2 - z1 * z2
            x = w1 * x2 + x1 * w2 + y1 * z2 - z1 * y2
            y = w1 * y2 - x1 * z2 + y1 * w2 + z1 * x2
            z = w1 * z2 + x1 * y2 - y1 * x2 + z1 * w2
            return jnp.stack([w, x, y, z], axis=-2)

        def _normalize(q):
            return q / jnp.sqrt(jnp.sum(q * q, axis=0, keepdims=True) + EPS)
        key = jax.random.key(seed)
        k1, k2, k3, k4 = jax.random.split(key, 4)
        B, T, d_model = (4, 1024, 256)
        quat_dim = d_model // 4
        x = jax.random.normal(k1, (B, T, d_model), dtype=jnp.float32)
        q_left = jax.random.normal(k2, (4, quat_dim), dtype=jnp.float32)
        q_right = jax.random.normal(k3, (4, quat_dim), dtype=jnp.float32)
        spectral_gate = jax.random.uniform(k4, (1, 1, 1, quat_dim), dtype=jnp.float32)
        return {'x': x, 'q_left': q_left, 'q_right': q_right, 'spectral_gate': spectral_gate}
    _L1_cond_all = _L1_cond_setup()
    _L1_cond_in = {k: v for k, v in _L1_cond_all.items() if k in ('q_right', 'spectral_gate')}
    del _L1_cond_all

    def _L1_ffn_setup():
        import jax, jax.numpy as jnp
        import numpy as np
        DIM = 256
        DEPTH = 2
        HEADS = 8
        DIM_HEAD = 64
        WINDOW = 128
        INNER = HEADS * DIM_HEAD
        HID = int(DIM * 4 * 2 / 3)
        B, N = (2, 2048)
        QK_SCALE = 8.0

        def shift_token(t):
            t1, t2 = jnp.split(t, 2, axis=-1)
            t2 = jnp.pad(t2, ((0, 0), (1, 0), (0, 0)))[:, :-1]
            return jnp.concatenate([t1, t2], axis=-1)

        def l2norm(t):
            return t / jnp.clip(jnp.linalg.norm(t, axis=-1, keepdims=True), 1e-12)

        def rotate_half(x):
            x1, x2 = jnp.split(x, 2, axis=-1)
            return jnp.concatenate([-x2, x1], axis=-1)

        def rotary_xpos(q, k):
            n = q.shape[-2]
            half_idx = jnp.arange(0, DIM_HEAD, 2, dtype=jnp.float32)
            inv_freq = 1.0 / 10000.0 ** (half_idx / DIM_HEAD)
            t = jnp.arange(n, dtype=jnp.float32)
            freqs = t[:, None] * inv_freq[None, :]
            freqs = jnp.concatenate([freqs, freqs], axis=-1)
            base = (half_idx + 0.4 * DIM_HEAD) / (1.4 * DIM_HEAD)
            power = (t - n // 2) / float(WINDOW // 2)
            scale = base[None, :] ** power[:, None]
            scale = jnp.concatenate([scale, scale], axis=-1)
            cos, sin = (jnp.cos(freqs), jnp.sin(freqs))
            q = q * cos * scale + rotate_half(q) * sin * scale
            k = k * cos / scale + rotate_half(k) * sin / scale
            return (q, k)

        def local_attention(q, k, v):
            b, h, n, d = q.shape
            w = n // WINDOW
            bq = q.reshape(b, h, w, WINDOW, d) * QK_SCALE
            bk = k.reshape(b, h, w, WINDOW, d)
            bv = v.reshape(b, h, w, WINDOW, d)

            def look_around(t):
                p = jnp.pad(t, ((0, 0), (0, 0), (1, 0), (0, 0), (0, 0)))
                return jnp.concatenate([p[:, :, :w], p[:, :, 1:]], axis=3)
            bk, bv = (look_around(bk), look_around(bv))
            bt = jnp.arange(n).reshape(w, WINDOW)
            btp = jnp.pad(bt, ((1, 0), (0, 0)), constant_values=-1)
            btk = jnp.concatenate([btp[:w], btp[1:]], axis=1)
            sim = jnp.einsum('bhwid,bhwjd->bhwij', bq, bk)
            i = bt[:, :, None]
            j = btk[:, None, :]
            mask = (i < j) | (i > j + WINDOW) | (j == -1)
            sim = jnp.where(mask, -jnp.finfo(sim.dtype).max, sim)
            attn = jax.nn.softmax(sim, axis=-1)
            out = jnp.einsum('bhwij,bhwjd->bhwid', attn, bv)
            return out.reshape(b, h, n, d)

        def _layer(x, wqkv, qs, ksc, wo, lg, lb, w1, b1, w2, b2):
            b, n, _ = x.shape
            h = shift_token(x)
            qkv = h @ wqkv
            q, k, v = jnp.split(qkv, 3, axis=-1)
            to_heads = lambda t: t.reshape(b, n, HEADS, DIM_HEAD).transpose(0, 2, 1, 3)
            q, k, v = (to_heads(q), to_heads(k), to_heads(v))
            q = l2norm(q) * qs
            k = l2norm(k) * ksc
            q, k = rotary_xpos(q, k)
            o = local_attention(q, k, v)
            o = o.transpose(0, 2, 1, 3).reshape(b, n, INNER)
            x = x + o @ wo
            h = shift_token(x)
            mu = h.mean(-1, keepdims=True)
            var = h.var(-1, keepdims=True)
            h = (h - mu) / jnp.sqrt(var + 1e-05) * lg + lb
            h = h @ w1 + b1
            a, g = jnp.split(h, 2, axis=-1)
            h = a * jax.nn.gelu(g, approximate=False)
            x = x + h @ w2 + b2
            return x
        key = jax.random.key(seed)
        ks = jax.random.split(key, 6)
        return {'x': jax.random.normal(ks[0], (B, N, DIM), jnp.float32), 'wqkv': jax.random.normal(ks[1], (DEPTH, DIM, 3 * INNER), jnp.float32) * 0.02, 'q_scale': jnp.ones((DEPTH, DIM_HEAD), jnp.float32), 'k_scale': jnp.ones((DEPTH, DIM_HEAD), jnp.float32), 'wo': jax.random.normal(ks[2], (DEPTH, INNER, DIM), jnp.float32) * 0.02, 'ln_g': jnp.ones((DEPTH, DIM), jnp.float32), 'ln_b': jnp.zeros((DEPTH, DIM), jnp.float32), 'w1': jax.random.normal(ks[3], (DEPTH, DIM, 2 * HID), jnp.float32) * 0.02, 'b1': jnp.zeros((DEPTH, 2 * HID), jnp.float32), 'w2': jax.random.normal(ks[4], (DEPTH, HID, DIM), jnp.float32) * 0.02, 'b2': jnp.zeros((DEPTH, DIM), jnp.float32)}
    _L1_ffn_all = _L1_ffn_setup()
    _L1_ffn_in = {k: v for k, v in _L1_ffn_all.items() if k in ('wqkv', 'q_scale', 'k_scale', 'wo', 'ln_g', 'ln_b', 'w1', 'b1', 'w2', 'b2')}
    del _L1_ffn_all
    return {'x': x, 'cond_256': cond_256, 'cond_64': cond_64, 'L0_cond_input_basis': _L0_cond_in['input_basis'], 'L0_cond_mode_to_rank': _L0_cond_in['mode_to_rank'], 'L0_cond_output_basis': _L0_cond_in['output_basis'], 'L0_ffn_router_w': _L0_ffn_in['router_w'], 'L0_ffn_w1': _L0_ffn_in['w1'], 'L0_ffn_w2': _L0_ffn_in['w2'], 'L1_cond_q_right': _L1_cond_in['q_right'], 'L1_cond_spectral_gate': _L1_cond_in['spectral_gate'], 'L1_ffn_wqkv': _L1_ffn_in['wqkv'], 'L1_ffn_q_scale': _L1_ffn_in['q_scale'], 'L1_ffn_k_scale': _L1_ffn_in['k_scale'], 'L1_ffn_wo': _L1_ffn_in['wo'], 'L1_ffn_ln_g': _L1_ffn_in['ln_g'], 'L1_ffn_ln_b': _L1_ffn_in['ln_b'], 'L1_ffn_w1': _L1_ffn_in['w1'], 'L1_ffn_b1': _L1_ffn_in['b1'], 'L1_ffn_w2': _L1_ffn_in['w2'], 'L1_ffn_b2': _L1_ffn_in['b2']}

def reference(x, cond_256, cond_64, L0_cond_input_basis, L0_cond_mode_to_rank, L0_cond_output_basis, L0_ffn_router_w, L0_ffn_w1, L0_ffn_w2, L1_cond_q_right, L1_cond_spectral_gate, L1_ffn_wqkv, L1_ffn_q_scale, L1_ffn_k_scale, L1_ffn_wo, L1_ffn_ln_g, L1_ffn_ln_b, L1_ffn_w1, L1_ffn_b1, L1_ffn_w2, L1_ffn_b2):
    import jax
    import jax.numpy as jnp

    def _L0_cond_ref(x, spectral_coeff, rank_coeff, input_basis, mode_to_rank, output_basis):
        import math
        import jax, jax.numpy as jnp
        import numpy as np
        from jax.scipy.linalg import cholesky, solve_triangular
        B, S, D, O, K, R = (4, 2048, 256, 256, 64, 64)

        def build_dct_basis(dim: int, num_bases: int) -> np.ndarray:
            num_bases = min(num_bases, dim)
            positions = np.arange(dim, dtype=np.float32)[None, :]
            modes = np.arange(num_bases, dtype=np.float32)[:, None]
            basis = np.cos(math.pi / float(dim) * (positions + 0.5) * modes)
            basis[0] = basis[0] / math.sqrt(2.0)
            basis = basis * math.sqrt(2.0 / float(dim))
            return basis.astype(np.float32)

        def _orthogonalize_mode_to_rank(raw: jnp.ndarray) -> jnp.ndarray:
            raw = raw.astype(jnp.float32)
            gram = raw.T @ raw
            eye = jnp.eye(raw.shape[1], dtype=jnp.float32)
            chol = cholesky(gram + 0.0001 * eye, lower=True)
            inv_chol = solve_triangular(chol, eye, lower=True)
            q = raw @ inv_chol.T
            signs = jnp.sign(jnp.sum(q * raw, axis=0, keepdims=True))
            signs = jnp.where(signs == 0, jnp.ones_like(signs), signs)
            return q * signs
        mtr = _orthogonalize_mode_to_rank(mode_to_rank).astype(x.dtype)
        proj = jnp.einsum('bsd,kd->bsk', x, input_basis.astype(x.dtype))
        proj = proj * spectral_coeff[:, None, :]
        hidden = jnp.einsum('bsk,kr->bsr', proj, mtr)
        hidden = hidden * rank_coeff[:, None, :]
        out = jnp.einsum('bsr,ro->bso', hidden, output_basis.astype(x.dtype))
        return out

    def _L0_ffn_ref(hidden_states, router_w, w1, w2):
        import jax, jax.numpy as jnp
        import numpy as np
        EPS = 1e-09
        TOP_K = 2
        orig_shape = hidden_states.shape
        H = orig_shape[-1]
        E = router_w.shape[-1]
        flat = hidden_states.reshape(-1, H)
        T = flat.shape[0]
        gate_logits = flat @ router_w
        gate_probs = jax.nn.softmax(gate_logits, axis=-1)
        topk_w, topk_idx = jax.lax.top_k(gate_probs, TOP_K)
        topk_w = topk_w / jnp.clip(topk_w.sum(-1, keepdims=True), EPS)
        cw = jnp.zeros((T, E), dtype=flat.dtype).at[jnp.arange(T)[:, None], topk_idx].add(topk_w)
        h = jax.nn.silu(jnp.einsum('td,edf->etf', flat, w1))
        y = jnp.einsum('etf,efd->etd', h, w2)
        out = jnp.einsum('etd,te->td', y, cw)
        return out.reshape(orig_shape)

    def _L1_cond_ref(x, q_left, q_right, spectral_gate):
        import jax, jax.numpy as jnp
        import numpy as np
        EPS = 1e-08

        def hamilton(q1, q2):
            w1, x1, y1, z1 = (q1[..., i, :] for i in range(4))
            w2, x2, y2, z2 = (q2[..., i, :] for i in range(4))
            w = w1 * w2 - x1 * x2 - y1 * y2 - z1 * z2
            x = w1 * x2 + x1 * w2 + y1 * z2 - z1 * y2
            y = w1 * y2 - x1 * z2 + y1 * w2 + z1 * x2
            z = w1 * z2 + x1 * y2 - y1 * x2 + z1 * w2
            return jnp.stack([w, x, y, z], axis=-2)

        def _normalize(q):
            return q / jnp.sqrt(jnp.sum(q * q, axis=0, keepdims=True) + EPS)
        B, T, d_model = x.shape
        quat_dim = d_model // 4
        x_quat = x.reshape(B, T, 4, quat_dim)
        x_spectral = jnp.fft.fft(x_quat, axis=1)
        x_filtered = jnp.fft.ifft(x_spectral * spectral_gate, axis=1).real.astype(x.dtype)
        q_left_n = _normalize(q_left)
        q_right_n = _normalize(q_right)
        conj_sign = jnp.array([1.0, -1.0, -1.0, -1.0], dtype=x.dtype)[:, None]
        q_right_conj = q_right_n * conj_sign
        x_right = hamilton(x_filtered, q_right_conj)
        x_rotated = hamilton(q_left_n, x_right)
        return x_rotated.reshape(B, T, d_model)

    def _L1_ffn_ref(x, wqkv, q_scale, k_scale, wo, ln_g, ln_b, w1, b1, w2, b2):
        import jax, jax.numpy as jnp
        import numpy as np
        DIM = 256
        DEPTH = 2
        HEADS = 8
        DIM_HEAD = 64
        WINDOW = 128
        INNER = HEADS * DIM_HEAD
        HID = int(DIM * 4 * 2 / 3)
        B, N = (2, 2048)
        QK_SCALE = 8.0

        def shift_token(t):
            t1, t2 = jnp.split(t, 2, axis=-1)
            t2 = jnp.pad(t2, ((0, 0), (1, 0), (0, 0)))[:, :-1]
            return jnp.concatenate([t1, t2], axis=-1)

        def l2norm(t):
            return t / jnp.clip(jnp.linalg.norm(t, axis=-1, keepdims=True), 1e-12)

        def rotate_half(x):
            x1, x2 = jnp.split(x, 2, axis=-1)
            return jnp.concatenate([-x2, x1], axis=-1)

        def rotary_xpos(q, k):
            n = q.shape[-2]
            half_idx = jnp.arange(0, DIM_HEAD, 2, dtype=jnp.float32)
            inv_freq = 1.0 / 10000.0 ** (half_idx / DIM_HEAD)
            t = jnp.arange(n, dtype=jnp.float32)
            freqs = t[:, None] * inv_freq[None, :]
            freqs = jnp.concatenate([freqs, freqs], axis=-1)
            base = (half_idx + 0.4 * DIM_HEAD) / (1.4 * DIM_HEAD)
            power = (t - n // 2) / float(WINDOW // 2)
            scale = base[None, :] ** power[:, None]
            scale = jnp.concatenate([scale, scale], axis=-1)
            cos, sin = (jnp.cos(freqs), jnp.sin(freqs))
            q = q * cos * scale + rotate_half(q) * sin * scale
            k = k * cos / scale + rotate_half(k) * sin / scale
            return (q, k)

        def local_attention(q, k, v):
            b, h, n, d = q.shape
            w = n // WINDOW
            bq = q.reshape(b, h, w, WINDOW, d) * QK_SCALE
            bk = k.reshape(b, h, w, WINDOW, d)
            bv = v.reshape(b, h, w, WINDOW, d)

            def look_around(t):
                p = jnp.pad(t, ((0, 0), (0, 0), (1, 0), (0, 0), (0, 0)))
                return jnp.concatenate([p[:, :, :w], p[:, :, 1:]], axis=3)
            bk, bv = (look_around(bk), look_around(bv))
            bt = jnp.arange(n).reshape(w, WINDOW)
            btp = jnp.pad(bt, ((1, 0), (0, 0)), constant_values=-1)
            btk = jnp.concatenate([btp[:w], btp[1:]], axis=1)
            sim = jnp.einsum('bhwid,bhwjd->bhwij', bq, bk)
            i = bt[:, :, None]
            j = btk[:, None, :]
            mask = (i < j) | (i > j + WINDOW) | (j == -1)
            sim = jnp.where(mask, -jnp.finfo(sim.dtype).max, sim)
            attn = jax.nn.softmax(sim, axis=-1)
            out = jnp.einsum('bhwij,bhwjd->bhwid', attn, bv)
            return out.reshape(b, h, n, d)

        def _layer(x, wqkv, qs, ksc, wo, lg, lb, w1, b1, w2, b2):
            b, n, _ = x.shape
            h = shift_token(x)
            qkv = h @ wqkv
            q, k, v = jnp.split(qkv, 3, axis=-1)
            to_heads = lambda t: t.reshape(b, n, HEADS, DIM_HEAD).transpose(0, 2, 1, 3)
            q, k, v = (to_heads(q), to_heads(k), to_heads(v))
            q = l2norm(q) * qs
            k = l2norm(k) * ksc
            q, k = rotary_xpos(q, k)
            o = local_attention(q, k, v)
            o = o.transpose(0, 2, 1, 3).reshape(b, n, INNER)
            x = x + o @ wo
            h = shift_token(x)
            mu = h.mean(-1, keepdims=True)
            var = h.var(-1, keepdims=True)
            h = (h - mu) / jnp.sqrt(var + 1e-05) * lg + lb
            h = h @ w1 + b1
            a, g = jnp.split(h, 2, axis=-1)
            h = a * jax.nn.gelu(g, approximate=False)
            x = x + h @ w2 + b2
            return x
        for l in range(DEPTH):
            x = _layer(x, wqkv[l], q_scale[l], k_scale[l], wo[l], ln_g[l], ln_b[l], w1[l], b1[l], w2[l], b2[l])
        return x
    x = x + _L0_ffn_ref(_L0_cond_ref(x, cond_256, cond_64, L0_cond_input_basis, L0_cond_mode_to_rank, L0_cond_output_basis), L0_ffn_router_w, L0_ffn_w1, L0_ffn_w2)
    x = x + _L1_ffn_ref(_L1_cond_ref(x, cond_256, L1_cond_q_right, L1_cond_spectral_gate), L1_ffn_wqkv, L1_ffn_q_scale, L1_ffn_k_scale, L1_ffn_wo, L1_ffn_ln_g, L1_ffn_ln_b, L1_ffn_w1, L1_ffn_b1, L1_ffn_w2, L1_ffn_b2)
    return x

_drawn_inputs = setup_inputs


def setup_inputs(seed=0):
    import zlib

    import numpy as np

    out = dict(_drawn_inputs(seed))
    spreads = {'L1_ffn_q_scale': (1.0, 0.6),
     'L1_ffn_k_scale': (1.0, 0.6),
     'L1_ffn_ln_g': (1.0, 0.6),
     'L1_ffn_ln_b': (0.0, 2.0),
     'L1_ffn_b1': (0.0, 2.0),
     'L1_ffn_b2': (0.0, 0.8)}
    factors = {'cond_64': 6.832,
     'L0_cond_input_basis': 7.039,
     'L0_cond_mode_to_rank': 7.321,
     'L0_cond_output_basis': 6.902,
     'L0_ffn_router_w': 8.0,
     'L0_ffn_w1': 6.968,
     'L0_ffn_w2': 6.94,
     'L1_ffn_wqkv': 2.821,
     'L1_ffn_wo': 2.952,
     'L1_ffn_w1': 8.0,
     'L1_ffn_w2': 8.0}
    for name, (base, spread) in spreads.items():
        noise = np.random.default_rng([zlib.crc32(name.encode()), seed]).standard_normal(out[name].shape)
        drawn = base * np.exp(spread * noise) if base else spread * noise
        out[name] = jnp.asarray(drawn.astype(out[name].dtype))
    for name, factor in factors.items():
        out[name] = (out[name] * factor).astype(out[name].dtype)
    return out
```

```python
from contextlib import ExitStack

import concourse.bass as bass
from concourse import mybir
from concourse.alu_op_type import AluOpType as ALU
import numpy as np

F32 = mybir.dt.float32
BF16 = mybir.dt.bfloat16
U32 = mybir.dt.uint32
ACT = mybir.ActivationFunctionType
AX = mybir.AxisListType

P = 128
B, T, D = 8, 512, 256
DC = D // P
NW = T // P
K = 64
E, F = 8, 512
FC = F // P
L = 2
H, DH = 8, 64
INNER = H * DH
IC = INNER // P
HID = D * 4 * 2 // 3
HJ = [min(P, HID - j * P) for j in range((HID + P - 1) // P)]
NJ = len(HJ)
MASKED = -1.0e30
LN_EPS = 1e-5
NORM_FLOOR = 1e-24
LN_SHIFT = 2.0 ** 20



class Counter:
    def __init__(self, start=None):
        self.n = dict(start or {})

    def take(self, name, k):
        v = self.n.get(name, 0)
        self.n[name] = v + k
        return v


def window_start(s, l, w):
    return [dict(kind=kind, s=s, l=l, w=w) for kind in ("qkv", "norm", "turn")]


def attention_steps(s, l, after):
    out = []
    for w in range(NW):
        def st(kind, g=None, w=w):
            return dict(kind=kind, s=s, l=l, w=w, g=g)
        following = window_start(s, l, w + 1) if w + 1 < NW else window_start(*after, 0) if after else []
        qkv, norm, turn = ([x] for x in following) if following else ([], [], [])
        out += [st("score", 0), st("score", 1)]
        if w:
            out.append(st("turn_o", w=w - 1))
        out += qkv + [st("turn_p", 0), st("score", 2), st("turn_p", 1)] + norm
        out += [st("pv", 0), st("score", 3), st("turn_p", 2), st("pv", 1)] + turn
        out += [st("turn_p", 3), st("pv", 2), st("pv", 3)]
    return out + [dict(kind="turn_o", s=s, l=l, w=NW - 1)]


def ffn_steps(s, l):
    def st(kind, **kw):
        return dict(kind=kind, s=s, l=l, **kw)
    out = [st("wo", c=c) for c in range(DC)] + [st("mean"), st("var"), st("hnorm")]
    out += [st("gate", j=j) for j in range(NJ)] + [st("gelu")]
    out += [st("value", j=j) for j in range(NJ)] + [st("down", c=c) for c in range(DC)]
    return out


def load_steps(s):
    return [dict(kind="load", s=s), dict(kind="rotate", s=s)]


def out_steps(s):
    return [dict(kind="out", s=s)]


def merge(attention, other, upto):
    out, j = [], 0
    for i, x in enumerate(attention):
        out.append(x)
        while j < len(other) and (i + 1 >= upto or (j + 1) * upto <= (i + 1) * len(other)):
            out.append(other[j])
            j += 1
    assert j == len(other)
    return out


def before_next(attention):
    return max(i for i, x in enumerate(attention) if x["kind"] == "qkv")


def head_of(g, hh):
    return 4 * (g // 2) + g % 2 + 2 * hh


USES = dict(qkv=3, turn=2, turn_o=1, wo=1, mean=1, var=1, gate=1, value=1, down=1, load=DC, rotate=DC, out=2)


def number(steps, c):
    out = []
    for st in steps:
        st = dict(st)
        kind, s = st["kind"], st["s"]
        st["use"] = c.take("use", USES.get(kind, 0))
        if kind in ("qkv", "norm", "turn", "turn_o"):
            st["win"] = c.take("win_" + kind, 1)
        if kind in ("score", "turn_p", "pv"):
            st["grp"] = c.take("grp_" + kind, 1)
            st["win"] = st["grp"] // 4
        st["ffn"] = c.take("ffn", kind == "down" and st["c"] == DC - 1)
        st["load"] = c.take("load", kind == "load")
        st["outs"] = c.take("outs", kind == "out")
        for what in ("turn", "turn_o", "wo", "gate", "value", "load"):
            st[what + "_use"] = c.n.get("last_" + what)
        st["x_use"] = c.n.get(f"last_x{s}")
        if kind in USES:
            c.n["last_" + kind] = st["use"] + USES[kind] - 1
        if kind in ("rotate", "down"):
            c.n[f"last_x{s}"] = c.n["last_" + kind]
        out.append(st)
    return out


def schedule():
    def section(att, after, other):
        steps = attention_steps(*att, after)
        return merge(steps, other, before_next(steps) if after else len(steps) - 1)

    c = Counter()
    first = number(load_steps(0) + window_start(0, 0, 0) + section((0, 0), (1, 0), load_steps(1)), c)
    start = dict(c.n)
    front = (section((1, 0), (0, 1), ffn_steps(0, 0)) + section((0, 1), (1, 1), ffn_steps(1, 0)))
    third = section((1, 1), (0, 0), ffn_steps(0, 1) + out_steps(0) + load_steps(0))
    fourth = section((0, 0), (1, 0), ffn_steps(1, 1) + out_steps(1) + load_steps(1))
    body = number(front + third + fourth, c)
    per = {k: c.n[k] - start.get(k, 0) for k in c.n if not k.startswith("last_")}
    for what in ("turn", "turn_o"):
        assert c.n["last_" + what] - start["last_" + what] == per["use"]
    last = number(front + section((1, 1), None, ffn_steps(0, 1) + out_steps(0))
                  + ffn_steps(1, 1) + out_steps(1), Counter(start))
    return first, body, last, per


def build(nc, x, cond_256, cond_64, L0_cond_input_basis, L0_cond_mode_to_rank, L0_cond_output_basis,
          L0_ffn_router_w, L0_ffn_w1, L0_ffn_w2, L1_cond_q_right, L1_cond_spectral_gate,
          L1_ffn_wqkv, L1_ffn_q_scale, L1_ffn_k_scale, L1_ffn_wo, L1_ffn_ln_g, L1_ffn_ln_b,
          L1_ffn_w1, L1_ffn_b1, L1_ffn_w2, L1_ffn_b2, rotary, out):
    first, body, last, per = schedule()
    NP = 3
    USE, WIN, GRP, FFN, OUTS = per["use"], per["win_qkv"], per["grp_pv"], per["ffn"], per["outs"]
    LOADS = per["load"]
    assert USE % NP == 0 and WIN % 4 == 0 and GRP % 4 == 0
    ITER = B // 2
    x1 = nc.dram_tensor("x_after_moe", [B, P, NW, D], F32, kind="Internal").ap()

    with ExitStack() as whole:
        def scope(stack):
            return (lambda name, shape, dt=F32: stack.enter_context(nc.sbuf_tensor(name, shape, dt)),
                    lambda name, shape, dt=F32: stack.enter_context(nc.psum_tensor(name, shape, dt)),
                    lambda name: stack.enter_context(nc.semaphore(name)))

        sb, _, sem = scope(whole)
        ident = sb("ident", [P, P])
        ones = sb("ones", [P, P])
        mean_w = sb("mean_w", [P, P])
        ident_bf = sb("ident_bf", [P, P], BF16)
        mask = sb("mask", [P, 2, 2, 2 * P], BF16)
        tabs = sb("tabs", [P, L, 4, NW, DH])
        rot = sb("rot", [P, DC, D])
        wqkv = sb("wqkv", [P, L, DC, 3 * INNER])
        wo = sb("wo", [P, L, IC, D])
        w1 = sb("w1", [P, L, DC, 2 * HID])
        w2 = sb("w2", [P, L, NJ, D])
        lng = sb("lng", [P, L, DC])
        b1 = sb("b1", [P, L, 2, NJ])
        b2 = sb("b2", [P, L, DC])
        consts = sb("consts", [P, 4])
        layer_weights = sem("layer_weights")

        with ExitStack() as st:
            sb, ps, sem = scope(st)
            w1m = sb("w1m", [P, E, DC, F])
            w2m = sb("w2m", [P, E, FC, D])
            rw = sb("rw", [P, DC, E])
            basis = sb("basis", [K, D])
            basisT = sb("basisT", [P, DC, K])
            raw = sb("raw", [K, K])
            rawT = sb("rawT", [K, K])
            outb = sb("outb", [K, D])
            c256 = sb("c256", [P, B])
            c64 = sb("c64", [K, B])
            aug = sb("aug", [K, 2 * K])
            row = sb("row", [K, 2 * K])
            below = sb("below", [K, K])
            small = sb("small", [K, 16])
            UT = sb("UT", [K, K])
            mtr = sb("mtr", [K, P])
            pace = sb("pace", [P, 8])
            prod = sb("prod", [K, K])
            srow = sb("srow", [K, 1])
            qr = sb("qr", [P, 4])
            nql = sb("nql", [P, 4])
            nqr = sb("nqr", [P, 4])
            ql = sb("ql", [P, 4])
            gate = sb("gate", [P, 1])
            ss = sb("ss", [P, 8])
            sq8 = sb("sq8", [P, B])
            Lm = sb("Lm", [P, 4, 4])
            Rm = sb("Rm", [P, 4, 4])
            coef = sb("coef", [P, 4, 4])
            cterm = sb("cterm", [P, 4, 4])
            rtab = sb("rtab", [P, 4, NW, DH])
            sc = sb("sc", [P, L, 4, DH])
            lnb = sb("lnb", [P, L, DC])
            b1raw = sb("b1raw", [P, L, 2, NJ])
            iota_i = sb("iota_i", [P, E], mybir.dt.int32)
            iota8 = sb("iota8", [P, E])
            xin = sb("xin", [P, NW, D])
            acc = sb("acc", [P, NW, D])
            xT = sb("xTa", [P, DC, T])
            projT = sb("projT", [K, T])
            hidT = sb("hidT", [K, T])
            xoT = sb("xoT", [P, DC, T])
            lg = sb("lg", [P, NW, E])
            m8 = sb("m8", [P, NW, 8])
            i8 = sb("i8", [P, NW, 8], U32)
            i8f = sb("i8f", [P, NW, 2])
            gap = sb("gap", [P, NW])
            eg = sb("eg", [P, NW])
            den = sb("den", [P, NW])
            wt = sb("wt", [P, NW, 2])
            hit = sb("hit", [P, 2, NW, E])
            cw = sb("cw", [P, NW, E])
            tanh = sb("tanh", [P, 3, F])
            hp = sb("hp", [P, 2, FC, T])

            hb = [ps(f"hb{i}", [P, 512]) for i in range(3)]
            yb = [ps(f"yb{i}", [P, 2, D]) for i in range(4)]
            pm = ps("pm", [P, 512])

            small_in = sem("small_in")
            expert_w = sem("expert_w")
            made = sem("made")
            filled = sem("filled")
            pe_prep = sem("pe_prep")
            v_prep = sem("v_prep")
            a_prep = sem("a_prep")
            x_in = sem("x_in")
            stored = sem("stored")
            h_full = sem("h_full")
            h_taken = [sem(f"h_taken{i}") for i in range(3)]
            tanh_done = sem("tanh_done")
            y_full = sem("y_full")
            y_taken = sem("y_taken")
            small_b = sem("small_b")
            chain = sem("chain")
            exp_done = sem("exp_done_a")
            gap_done = sem("gap_done")

            N_SMALL = 27
            PREP_QN = 3 + 3 * K + 15
            HU = 7 + 4 * E
            assert HU % 3 == 0
            XCH = x.rearrange("b (w p) d -> b p w d", p=P)

            with nc.Block() as block:
                @block.sync
                def _(sp):
                    n = [0]

                    def small_load(dst, src, eng=sp):
                        eng.dma_start(dst, src, allow_slow_non_contiguous=True).then_inc(small_in, 16)
                        n[0] += 1
                    small_load(raw[:, :], L0_cond_mode_to_rank)
                    for half in range(2):
                        small_load(c256[half * K:(half + 1) * K, :], cond_256.rearrange("b k -> k b"))
                        small_load(qr[half * K:(half + 1) * K, :], L1_cond_q_right.rearrange("q k -> k q"))
                        small_load(gate[half * K:(half + 1) * K, :],
                                   L1_cond_spectral_gate.rearrange("a b c k -> k (a b c)"))
                    small_load(c64[:, :], cond_64.rearrange("b k -> k b"))
                    small_load(basis[:, :], L0_cond_input_basis)
                    small_load(outb[:, :], L0_cond_output_basis)
                    small_load(rw[:, :, :], L0_ffn_router_w.rearrange("(c p) e -> p c e", p=P))
                    small_load(rtab[:, :, :, :], rotary.rearrange("k (w p) d -> p k w d", p=P))
                    for l in range(L):
                        for kind, src in ((0, L1_ffn_q_scale), (2, L1_ffn_k_scale)):
                            small_load(sc[:, l, kind, :], src[l].partition_broadcast(P))
                            small_load(sc[:, l, kind + 1, 0:DH // 2],
                                       src[l, DH // 2:DH].partition_broadcast(P))
                            small_load(sc[:, l, kind + 1, DH // 2:DH],
                                       src[l, 0:DH // 2].partition_broadcast(P))
                    small_load(lng[:, :, :], L1_ffn_ln_g.rearrange("l (c p) -> p l c", p=P))
                    small_load(lnb[:, :, :], L1_ffn_ln_b.rearrange("l (c p) -> p l c", p=P))
                    small_load(b2[:, :, :], L1_ffn_b2.rearrange("l (c p) -> p l c", p=P))
                    assert n[0] == N_SMALL, n[0]
                    sp.dma_start(xin[:, :, :], XCH[0]).then_inc(x_in, 16)
                    for e in range(E):
                        sp.dma_start(w1m[:, e, :, :], L0_ffn_w1[e].rearrange("(c p) f -> p c f", p=P)
                                     ).then_inc(expert_w, 16)
                        sp.dma_start(w2m[:, e, :, :], L0_ffn_w2[e].rearrange("(c p) d -> p c d", p=P)
                                     ).then_inc(expert_w, 16)
                    for l in range(L):
                        sp.dma_start(wqkv[:, l, :, :], L1_ffn_wqkv[l].rearrange("(c p) n -> p c n", p=P)
                                     ).then_inc(layer_weights, 16)
                        sp.dma_start(wo[:, l, :, :], L1_ffn_wo[l].rearrange("(c p) n -> p c n", p=P)
                                     ).then_inc(layer_weights, 16)
                        sp.dma_start(w1[:, l, :, :], L1_ffn_w1[l].rearrange("(c p) n -> p c n", p=P)
                                     ).then_inc(layer_weights, 16)
                        full = (NJ - 1) * P
                        sp.dma_start(w2[:, l, 0:NJ - 1, :], L1_ffn_w2[l, 0:full].rearrange("(j p) n -> p j n", p=P)
                                     ).then_inc(layer_weights, 16)
                        sp.dma_start(w2[0:HJ[-1], l, NJ - 1, :], L1_ffn_w2[l, full:HID]
                                     ).then_inc(layer_weights, 16)
                    with sp.Fori(0, B - 1) as b:
                        sp.wait_ge(y_taken, b * 2 * E + 3)
                        sp.dma_start(xin[:, :, :], XCH[b + 1]).then_inc(x_in, 16)
                        sp.wait_ge(y_taken, (b + 1) * 2 * E + 1)
                        sp.dma_start(x1[b], acc[:, :, :]).then_inc(stored, 16)
                    sp.wait_ge(y_taken, B * 2 * E + 1)
                    sp.dma_start(x1[B - 1], acc[:, :, :]).then_inc(stored, 16)
                    sp.wait_ge(stored, 16 * (B + 1))
                    sp.wait_ge(layer_weights, 16 * 5 * L)

                @block.gpsimd
                def _(pool):
                    pool.memset(ident[:, :], 0.0).then_inc(made, 1)
                    pool.memset(ones[:, :], 1.0).then_inc(made, 1)
                    pool.memset(below[:, :], 0.0).then_inc(made, 1)
                    pool.memset(mask[:, :, :, :], 0.0).then_inc(made, 1)
                    pool.iota(iota_i[:, :], [[1, E]], base=0, channel_multiplier=0).then_inc(made, 1)
                    pool.wait_ge(made, 5)
                    pool.affine_select(out=ident[:, :], in_=ident[:, :], compare_op=ALU.not_equal, fill=1.0,
                                       base=0, pattern=[[-1, P]], channel_multiplier=1).then_inc(made, 1)
                    pool.affine_select(out=below[:, :], in_=below[:, :], compare_op=ALU.is_ge, fill=-1.0,
                                       base=0, pattern=[[1, K]], channel_multiplier=-1).then_inc(made, 1)
                    for par in range(2):
                        cur = mask[:, par, :, par * P:(par + 1) * P]
                        prev = mask[:, par, :, (1 - par) * P:(2 - par) * P]
                        pool.affine_select(out=cur, in_=cur, compare_op=ALU.is_ge, fill=MASKED, base=0,
                                           pattern=[[0, 2], [-1, P]], channel_multiplier=1).then_inc(made, 1)
                        pool.affine_select(out=prev, in_=prev, compare_op=ALU.is_ge, fill=MASKED, base=0,
                                           pattern=[[0, 2], [1, P]], channel_multiplier=-1).then_inc(made, 1)
                N_MADE = 11

                @block.tensor
                def _(pe):
                    pe.wait_ge(small_in, 16 * N_SMALL)
                    pe.wait_ge(made, N_MADE)
                    n = [0]

                    def done(mm):
                        n[0] += 1
                        mm.then_inc(pe_prep, 1)
                    done(pe.matmul(pm[0:K, 0:K], raw[:, :], raw[:, :], start=True, stop=True))
                    done(pe.transpose(hb[0][0:K, 0:K], raw[:, :], ident[0:K, 0:K]))
                    for c in range(DC):
                        mm = pe.transpose(hb[1][:, c * K:(c + 1) * K], basis[:, c * P:(c + 1) * P], ident[0:K, 0:K])
                    done(mm)
                    assert n[0] == 3
                    for k in range(K):
                        pe.wait_ge(v_prep, 3 + 3 * k)
                        pe.matmul(pm[:, 0:2 * K], ident[0:K, k:k + 1].to_broadcast([K, P]), aug[:, :],
                                  start=True, stop=True).then_inc(pe_prep, 1)
                    base = 3 + 3 * K
                    pe.wait_ge(v_prep, base)
                    pe.transpose(pm[0:K, 0:K], aug[:, K:2 * K], ident[0:K, 0:K]).then_inc(pe_prep, 1)
                    pe.wait_ge(v_prep, base + 1)
                    pe.matmul(hb[0][0:K, 0:K], rawT[:, :], UT[:, :], start=True, stop=True).then_inc(pe_prep, 1)
                    pe.wait_ge(v_prep, base + 3)
                    pe.matmul(pm[0:K, 0:1], prod[:, :], ones[0:K, 0:1], start=True, stop=True).then_inc(pe_prep, 1)

                    def taken(u):
                        pe.wait_ge(h_taken[u[1] % 3], u[0] * (HU // 3) + u[1] // 3 + 2)

                    with pe.Fori(0, B) as b:
                        u = [0]

                        def bank():
                            k = u[0]
                            if k >= 3:
                                taken((b, k - 3))
                            else:
                                pe.wait_ge(h_taken[k], b * (HU // 3) + 1)
                            u[0] += 1
                            return hb[k % 3]
                        pe.wait_ge(x_in, 16 * (b + 1))
                        pe.wait_ge(v_prep, base + 8)
                        for c in range(DC):
                            o = bank()
                            for w in range(NW):
                                mm = pe.transpose(o[:, w * P:(w + 1) * P], xin[:, w, c * P:(c + 1) * P], ident[:, :])
                            mm.then_inc(h_full, 1)
                        taken((b, 0)); taken((b, 1))
                        o = bank()
                        for c in range(DC):
                            mm = pe.matmul(o[0:K, :], basisT[:, c, :], xT[:, c, :], start=(c == 0), stop=(c == DC - 1))
                        mm.then_inc(h_full, 1)
                        taken((b, 2))
                        o = bank()
                        pe.matmul(o[:, :], mtr[:, :], projT[:, :], start=True, stop=True).then_inc(h_full, 1)
                        taken((b, 3))
                        for c in range(DC):
                            o = bank()
                            pe.matmul(o[:, :], outb[:, c * P:(c + 1) * P], hidT[:, :], start=True, stop=True
                                      ).then_inc(h_full, 1)
                        taken((b, 4)); taken((b, 5))
                        o = bank()
                        for w in range(NW):
                            for c in range(DC):
                                mm = pe.matmul(o[:, w * E:(w + 1) * E], xoT[:, c, w * P:(w + 1) * P], rw[:, c, :],
                                               start=(c == 0), stop=(c == DC - 1))
                        mm.then_inc(h_full, 1)

                        def up(e):
                            pe.wait_ge(expert_w, 16 * 2 * E)
                            for j in range(FC):
                                o = bank()
                                for c in range(DC):
                                    mm = pe.matmul(o[:, :], w1m[:, e, c, j * P:(j + 1) * P], xoT[:, c, :],
                                                   start=(c == 0), stop=(c == DC - 1))
                                mm.then_inc(h_full, 1)

                        def down(e):
                            taken((b, 7 + 4 * e + 3))
                            for half in range(2):
                                m = 2 * e + half
                                if m >= 4:
                                    pe.wait_ge(y_taken, b * 2 * E + m - 2)
                                else:
                                    pe.wait_ge(y_taken, b * 2 * E + 1)
                                for k in range(2):
                                    w = 2 * half + k
                                    for j in range(FC):
                                        mm = pe.matmul(yb[m % 4][:, k, :], hp[:, e % 2, j, w * P:(w + 1) * P],
                                                       w2m[:, e, j, :], start=(j == 0), stop=(j == FC - 1))
                                mm.then_inc(y_full, 1)
                        up(0)
                        for e in range(1, E):
                            up(e)
                            down(e - 1)
                        down(E - 1)
                    pe.wait_ge(layer_weights, 16 * 5 * L)
                    pe.wait_ge(h_taken[(HU - 1) % 3], B * (HU // 3) + 1)
                    for l in range(L):
                        for side in range(2):
                            for j in range(NJ):
                                col = (l * 2 + side) * NJ + j
                                a = side * HID + j * P
                                for c in range(DC):
                                    mm = pe.matmul(pm[0:HJ[j], col:col + 1], w1[:, l, c, a:a + HJ[j]],
                                                   lnb[:, l, c:c + 1], start=(c == 0), stop=(c == DC - 1))
                    mm.then_inc(pe_prep, 1)

                @block.vector
                def _(v):
                    n = [0]

                    def step(ins):
                        n[0] += 1
                        ins.then_inc(v_prep, 1)
                        v.wait_ge(v_prep, n[0])
                    v.wait_ge(small_in, 16 * N_SMALL)
                    v.wait_ge(made, N_MADE)
                    v.wait_ge(pe_prep, 3)
                    v.tensor_copy(rawT[:, :], hb[0][0:K, 0:K])
                    v.tensor_copy(basisT[:, :, :], hb[1][:, 0:DC * K].rearrange("p (c k) -> p c k", c=DC))
                    v.tensor_copy(aug[:, K:2 * K], ident[0:K, 0:K])
                    step(v.tensor_scalar(prod[:, :], ident[0:K, 0:K], 1e-4, None, ALU.mult))
                    step(v.tensor_tensor(aug[:, 0:K], pm[0:K, 0:K], prod[:, :], ALU.add))
                    v.memset(mtr[:, K:P], 0.0)
                    for k, s in enumerate(h_taken + [y_taken]):
                        v.memset(pace[:, k:k + 1], 0.0).then_inc(s, 1)
                    v.memset(pace[:, 4:5], 0.0).then_inc(stored, 16)
                    step(v.memset(small[:, :], 0.0))
                    for k in range(K):
                        v.wait_ge(pe_prep, 3 + k + 1)
                        step(v.reciprocal(small[:, 0:1], pm[0:K, k:k + 1]))
                        step(v.tensor_scalar(small[:, 1:2], aug[:, k:k + 1], small[:, 0:1], below[:, k:k + 1],
                                             ALU.mult, ALU.mult))
                        step(v.scalar_tensor_tensor(aug[:, :], pm[0:K, 0:2 * K], small[:, 1:2], aug[:, :],
                                                    ALU.mult, ALU.add))
                    v.wait_ge(pe_prep, 3 + K + 1)
                    step(v.tensor_copy(UT[:, :], pm[0:K, 0:K]))
                    v.wait_ge(pe_prep, 3 + K + 2)
                    step(v.tensor_copy(mtr[:, 0:K], hb[0][0:K, 0:K]))
                    step(v.tensor_tensor(prod[:, :], mtr[:, 0:K], raw[:, :], ALU.mult))
                    step(v.tensor_tensor(row[:, 0:K], aug[:, 0:K], ident[0:K, 0:K], ALU.mult))
                    step(v.tensor_reduce(small[:, 2:3], row[:, 0:K], AX.X, ALU.add))
                    v.wait_ge(a_prep, 2)
                    step(v.tensor_scalar(small[:, 5:6], small[:, 4:5], small[:, 4:5], small[:, 2:3],
                                         ALU.mult, ALU.mult))
                    step(v.tensor_scalar(small[:, 6:7], small[:, 5:6], -0.5, 1.5, ALU.mult, ALU.add))
                    v.wait_ge(pe_prep, 3 + K + 3)
                    step(v.tensor_scalar(small[:, 7:8], pm[0:K, 0:1], 0.0, 2.0, ALU.is_ge, ALU.mult))
                    step(v.tensor_scalar(small[:, 8:9], small[:, 7:8], -1.0, small[:, 6:7], ALU.add, ALU.mult))
                    step(v.tensor_scalar(srow[:, :], small[:, 8:9], small[:, 4:5], None, ALU.mult))
                    v.tensor_scalar(mean_w[:, :], ones[:, :], 1.0 / D, None, ALU.mult)
                    v.tensor_copy(ident_bf[:, :], ident[:, :])
                    v.tensor_copy(iota8[:, :], iota_i[:, :])
                    for k, val in enumerate((LN_EPS, 10 * float(np.log(2.0)), 1e-8, 0.0)):
                        v.memset(consts[:, k:k + 1], val)
                    v.memset(b1[:, :, :, :], 0.0)
                    step(v.tensor_tensor(sq8[:, :], c256[:, :], c256[:, :], ALU.mult))
                    step(v.tensor_reduce(ss[:, 0:1], sq8[:, :], AX.X, ALU.add))
                    step(v.tensor_tensor(sq8[:, 0:4], qr[:, :], qr[:, :], ALU.mult))
                    step(v.tensor_reduce(ss[:, 1:2], sq8[:, 0:4], AX.X, ALU.add))
                    step(v.tensor_scalar(ss[:, 0:2], ss[:, 0:2], 1e-8, None, ALU.add))
                    QN = n[0]
                    v.wait_ge(a_prep, 4)
                    step(v.tensor_tensor(ss[:, 4:6], ss[:, 2:4], ss[:, 2:4], ALU.mult))
                    step(v.tensor_tensor(ss[:, 4:6], ss[:, 4:6], ss[:, 0:2], ALU.mult))
                    step(v.tensor_scalar(ss[:, 4:6], ss[:, 4:6], -0.5, 1.5, ALU.mult, ALU.add))
                    step(v.tensor_tensor(ss[:, 6:8], ss[:, 4:6], ss[:, 2:4], ALU.mult))
                    step(v.tensor_scalar(ql[:, :], c256[:, 0:4], ss[:, 6:7], None, ALU.mult))
                    step(v.tensor_scalar(qr[:, :], qr[:, :], ss[:, 7:8], gate[:, 0:1], ALU.mult, ALU.mult))
                    step(v.tensor_scalar(nql[:, :], ql[:, :], -1.0, None, ALU.mult))
                    step(v.tensor_scalar(nqr[:, :], qr[:, :], -1.0, None, ALU.mult))
                    W_, X_, Y_, Z_ = 0, 1, 2, 3
                    left = [[(1, W_), (-1, X_), (-1, Y_), (-1, Z_)], [(1, X_), (1, W_), (-1, Z_), (1, Y_)],
                            [(1, Y_), (1, Z_), (1, W_), (-1, X_)], [(1, Z_), (-1, Y_), (1, X_), (1, W_)]]
                    right = [[(1, W_), (-1, X_), (-1, Y_), (-1, Z_)], [(1, X_), (1, W_), (1, Z_), (-1, Y_)],
                             [(1, Y_), (-1, Z_), (1, W_), (1, X_)], [(1, Z_), (1, Y_), (-1, X_), (1, W_)]]
                    for o in range(4):
                        for m in range(4):
                            s_, q_ = left[o][m]
                            v.tensor_copy(Lm[:, m, o:o + 1], (ql if s_ > 0 else nql)[:, q_:q_ + 1])
                            s_, q_ = right[o][m]
                            s_ = s_ if q_ == W_ else -s_
                            last = v.tensor_copy(Rm[:, o, m:m + 1], (qr if s_ > 0 else nqr)[:, q_:q_ + 1])
                    step(last)
                    for m in range(4):
                        dst = coef if m == 0 else cterm
                        step(v.tensor_tensor(dst[:, :, :], Lm[:, m, :].unsqueeze(2).to_broadcast([P, 4, 4]),
                                             Rm[:, m, :].unsqueeze(1).to_broadcast([P, 4, 4]), ALU.mult))
                        if m:
                            step(v.tensor_tensor(coef[:, :, :], coef[:, :, :], cterm[:, :, :], ALU.add))
                    for c in range(DC):
                        for half in range(2):
                            p0 = half * K
                            for o in range(4):
                                v.tensor_scalar(rot[p0:p0 + K, c, o * K:(o + 1) * K], ident[p0:p0 + K, p0:p0 + K],
                                                coef[p0:p0 + K, o, 2 * c + half:2 * c + half + 1], None, ALU.mult)
                    for l in range(L):
                        for kind in range(4):
                            last = v.tensor_tensor(tabs[:, l, kind, :, :], rtab[:, kind, :, :],
                                                   sc[:, l, kind, :].unsqueeze(1).to_broadcast([P, NW, DH]), ALU.mult)
                    step(last)
                    assert QN == PREP_QN, QN

                    CH = 10
                    with v.Fori(0, B) as b:
                        m = [0]

                        def link(ins):
                            m[0] += 1
                            ins.then_inc(chain, 1)
                            v.wait_ge(chain, b * CH + m[0])

                        def full(k):
                            v.wait_ge(h_full, b * HU + k + 1)
                            return hb[k % 3]
                        o = full(2)
                        v.tensor_scalar(projT[:, :], o[0:K, :], c256[0:K, bass.ds(b, 1)], None, ALU.mult
                                        ).then_inc(h_taken[2], 1)
                        o = full(3)
                        v.tensor_scalar(hidT[:, :], o[0:K, :], c64[:, bass.ds(b, 1)], srow[:, 0:1], ALU.mult,
                                        ALU.mult).then_inc(h_taken[0], 1)
                        o = full(6)
                        v.tensor_copy(lg[:, :, :], o[:, 0:NW * E].rearrange("p (w e) -> p w e", w=NW)
                                      ).then_inc(h_taken[0], 1)
                        v.wait_ge(h_taken[0], b * (HU // 3) + 4)
                        v.memset(pace[:, 5:6], 0.0)
                        for w in range(NW):
                            last = v.max(m8[:, w, :], lg[:, w, :])
                        link(last)
                        v.memset(pace[:, 6:7], 0.0)
                        for w in range(NW):
                            last = v.max_index(i8[:, w, :], m8[:, w, :], lg[:, w, :])
                        link(last)
                        v.tensor_copy(i8f[:, :, :], i8[:, :, 0:2])
                        v.tensor_tensor(gap[:, :], m8[:, :, 1], m8[:, :, 0], ALU.subtract).then_inc(gap_done, 1)
                        v.wait_ge(exp_done, b + 1)
                        link(v.tensor_scalar(den[:, :], eg[:, :], 1.0, 2.0, ALU.add, ALU.mult))
                        link(v.reciprocal(wt[:, :, 0], den[:, :]))
                        link(v.tensor_tensor(wt[:, :, 1], eg[:, :], wt[:, :, 0], ALU.mult))
                        for k in range(2):
                            last = v.tensor_tensor(hit[:, k, :, :], iota8[:, :].unsqueeze(1).to_broadcast([P, NW, E]),
                                                   i8f[:, :, k:k + 1].to_broadcast([P, NW, E]), ALU.is_equal)
                            link(last)
                            last = v.tensor_tensor(hit[:, k, :, :], hit[:, k, :, :],
                                                   wt[:, :, k:k + 1].to_broadcast([P, NW, E]), ALU.mult)
                            link(last)
                        link(v.tensor_tensor(cw[:, :, :], hit[:, 0, :, :], hit[:, 1, :, :], ALU.add))
                        assert m[0] == CH, m[0]

                        def up(e):
                            if e >= 2:
                                v.wait_ge(y_full, b * 2 * E + 2 * (e - 1))
                            for j in range(FC):
                                k = 7 + 4 * e + j
                                v.wait_ge(tanh_done, b * FC * E + FC * e + j + 1)
                                v.scalar_tensor_tensor(hp[:, e % 2, j, :], tanh[:, (4 * e + j) % 3, :], 1.0,
                                                       hb[k % 3][:, :], ALU.add, ALU.mult).then_inc(h_taken[k % 3], 1)

                        def down(e):
                            if e == 0:
                                v.wait_ge(stored, 16 * b + 16)
                            for half in range(2):
                                q = 2 * e + half
                                v.wait_ge(y_full, b * 2 * E + q + 1)
                                if e:
                                    v.wait_ge(y_taken, b * 2 * E + q)
                                for k in range(2):
                                    w = 2 * half + k
                                    last = v.scalar_tensor_tensor(
                                        acc[:, w, :], yb[q % 4][:, k, :], cw[:, w, e:e + 1],
                                        (acc if e else xin)[:, w, :], ALU.mult, ALU.add)
                                last.then_inc(y_taken, 1)
                        up(0)
                        for e in range(1, E):
                            up(e)
                            down(e - 1)
                        down(E - 1)
                    v.wait_ge(pe_prep, 3 + K + 4)
                    v.wait_ge(small_b, 16 * 4 * L)
                    full_j = NJ - 1
                    pmv = pm[:, 0:2 * L * NJ].rearrange("p (l s j) -> p l s j", l=L, s=2)
                    v.tensor_tensor(b1[:, :, :, 0:full_j], pmv[:, :, :, 0:full_j], b1raw[:, :, :, 0:full_j], ALU.add)
                    v.tensor_tensor(b1[0:HJ[-1], :, :, full_j:NJ], pmv[0:HJ[-1], :, :, full_j:NJ],
                                    b1raw[0:HJ[-1], :, :, full_j:NJ], ALU.add)

                @block.scalar
                def _(a):
                    for l in range(L):
                        for side in range(2):
                            f = side * HID
                            full_j = (NJ - 1) * P
                            a.dma_start(b1raw[:, l, side, 0:NJ - 1],
                                        L1_ffn_b1[l, f:f + full_j].rearrange("(j p) -> p j", p=P),
                                        allow_slow_non_contiguous=True).then_inc(small_b, 16)
                            a.dma_start(b1raw[0:HJ[-1], l, side, NJ - 1:NJ],
                                        L1_ffn_b1[l, f + full_j:f + HID].rearrange("(p o) -> p o", o=1),
                                        allow_slow_non_contiguous=True).then_inc(small_b, 16)
                    a.preload_act_table_set("natural_log_exp_and_others")
                    base = 3 + 3 * K
                    a.wait_ge(v_prep, base + 5)
                    a.activation(small[:, 3:4], small[:, 2:3], ACT.Ln).then_inc(a_prep, 1)
                    a.wait_ge(a_prep, 1)
                    a.activation(small[:, 4:5], small[:, 3:4], ACT.Exp, scale=-0.5).then_inc(a_prep, 1)
                    a.wait_ge(v_prep, PREP_QN)
                    a.activation(ss[:, 2:4], ss[:, 0:2], ACT.Ln).then_inc(a_prep, 1)
                    a.wait_ge(a_prep, 3)
                    a.activation(ss[:, 2:4], ss[:, 2:4], ACT.Exp, scale=-0.5).then_inc(a_prep, 1)
                    a.preload_act_table_set("exp_and_others")
                    with a.Fori(0, B) as b:
                        for c in range(DC):
                            a.wait_ge(h_full, b * HU + c + 1)
                            a.copy(xT[:, c, :], hb[c][:, :]).then_inc(h_taken[c], 1)
                        for c in range(DC):
                            k = 4 + c
                            a.wait_ge(h_full, b * HU + k + 1)
                            a.copy(xoT[:, c, :], hb[k % 3][:, :]).then_inc(h_taken[k % 3], 1)
                        a.wait_ge(gap_done, b + 1)
                        a.activation(eg[:, :], gap[:, :], ACT.Exp).then_inc(exp_done, 1)
                        for e in range(E):
                            for j in range(FC):
                                k = 7 + 4 * e + j
                                a.wait_ge(h_full, b * HU + k + 1)
                                a.activation(tanh[:, (4 * e + j) % 3, :], hb[k % 3][:, :], ACT.Tanh, scale=0.5
                                             ).then_inc(tanh_done, 1)

        with ExitStack() as st:
            sb, ps, sem = scope(st)
            xT = [sb(f"xT{s}", [P, DC, T + 1]) for s in range(2)]
            x1tok = sb("x1tok", [P, NW, D])
            x1out = sb("x1out", [P, NW, D])
            outt = sb("outt", [P, NW, D])
            x1T = sb("x1T", [P, DC, T])
            raw = sb("qkraw", [P, 2, 2, INNER])
            qksq = sb("qksq", [P, 2 * INNER])
            ss = sb("ssum", [P, 2 * H])
            lns = sb("lns", [P, 2 * H])
            rn = sb("rn", [P, 2 * H])
            direct = sb("direct", [P, 2, INNER])
            swapped = sb("swapped", [P, 2, INNER])
            roped = sb("roped", [P, 2, INNER])
            vv = sb("vv", [P, 4, INNER])
            qT = sb("qT", [P, IC, P])
            kT = sb("kT", [P, IC, 2, P])
            nm = sb("nm", [P, 4, 2])
            prob = sb("prob", [P, 4, 2, 2 * P])
            rs = sb("rs", [P, 2, H])
            rr = sb("rr", [P, H])
            pT = sb("pT", [P, 4, 2, 2, P])
            on = sb("on", [P, INNER])
            oT = sb("oT", [P, IC, T])
            xc = sb("xc", [P, DC, T])
            xsq = sb("xsq", [P, DC, T])
            lnv = sb("lnv", [P, T])
            rstd = sb("rstd", [P, T])
            h = sb("h", [P, DC, T])
            gb = sb("gb", [P, NJ, T])
            hid = sb("hid", [P, NJ, T])

            pj = [ps(f"pj{i}", [P, 512]) for i in range(NP)]
            sc = [ps(f"sc{i}", [P, 2, 2 * P]) for i in range(2)]
            pt = [ps(f"pt{i}", [P, 2, 2, P]) for i in range(2)]
            ob = ps("ob", [P, INNER])

            proj_full = sem("proj_full")
            proj_taken = [sem(f"proj_taken{i}") for i in range(NP)]
            squared = sem("squared")
            edge = sem("edge")
            summed = sem("summed")
            floored = sem("floored")
            logged = sem("logged")
            norm_ready = sem("norm_ready")
            parts_ready = sem("parts_ready")
            added = sem("added")
            rope_done = sem("rope_done")
            s_full = sem("s_full")
            max_done = sem("max_done")
            exp_done = sem("exp_done")
            pt_full = sem("pt_full")
            pt_taken = [sem(f"pt_taken{i}") for i in range(2)]
            pv_done = sem("pv_done")
            inverted = sem("inverted")
            o_ready = sem("o_ready")
            xsq_ready = sem("xsq_ready")
            var_logged = sem("var_logged")
            rstd_ready = sem("rstd_ready")
            h_ready = sem("h_ready")
            gelu_done = sem("gelu_done")
            loaded = sem("loaded")
            reloaded = sem("reloaded")
            saved = sem("saved")

            def at(count, i, per_body, mul=1, add=0):
                return i * (per_body * mul) + (count * mul + add)

            def wait(eng, s, value):
                if not (isinstance(value, int) and value <= 0):
                    eng.wait_ge(s, value)

            def wait_taken(eng, u, i):
                eng.wait_ge(proj_taken[u % NP], at(u // NP, i, USE // NP, 1, 1))

            def wait_full(eng, u, i):
                eng.wait_ge(proj_full, at(u, i, USE, 1, 1))
                return pj[u % NP]

            def xs(s, c, t0=0, n=T):
                return xT[s][:, c, 1 - c + t0:1 - c + t0 + n]

            def walk(eng, one):
                for st in first:
                    one(st, 0)
                with eng.Fori(0, ITER - 1) as i:
                    for st in body:
                        one(st, i)
                for st in last:
                    one(st, ITER - 1)

            def move_p(eng, copy, st, i):
                g = st["grp"]
                n = 2 if st["w"] else 1
                eng.wait_ge(pt_full, at(g, i, GRP, 1, 1))
                wait(eng, pv_done, at(g, i, GRP, 1, -3))
                copy(pT[:, g % 4, :, 0:n, :], pt[g % 2][:, :, 0:n, :]).then_inc(pt_taken[g % 2], 1)

            with nc.Block() as block:
                @block.sync
                def _(sp):
                    def fetch(n):
                        sp.dma_start(x1tok[:, :, :], x1[n]).then_inc(loaded, 16)

                    def fetch_again(n):
                        sp.dma_start(x1out[:, :, :], x1[n]).then_inc(reloaded, 16)

                    def one(st, i, last_out=False):
                        if st["kind"] == "load" and st["load"] % 2 == 0:
                            wait_full(sp, st["use"] + 1, i)
                            fetch(i * 2 + (st["load"] + 1))
                        elif st["kind"] == "out":
                            wait_taken(sp, st["use"], i)
                            wait_taken(sp, st["use"] + 1, i)
                            sp.dma_start(out[i * 2 + st["outs"]].rearrange("(w p) d -> p w d", p=P), outt[:, :, :]
                                         ).then_inc(saved, 16)
                            if not last_out:
                                fetch_again(i * 2 + (st["outs"] + 1))
                    fetch(0)
                    fetch_again(0)
                    for st in first:
                        one(st, 0)
                    with sp.Fori(0, ITER - 1) as i:
                        wait_full(sp, body[0]["use"] - 1, i)
                        fetch(i * 2 + 2)
                        for st in body:
                            one(st, i)
                    for st in last:
                        one(st, ITER - 1, last_out=st["outs"] == OUTS - 1)
                    sp.wait_ge(saved, 16 * (B + 1))

                @block.tensor
                def _(pe):
                    pe.wait_ge(edge, 1)

                    def bank(u, i):
                        wait(pe, proj_taken[u % NP], at(u // NP, i, USE // NP))
                        return pj[u % NP]

                    def one(st, i):
                        kind, s, u = st["kind"], st["s"], st["use"]
                        l, w = st.get("l"), st.get("w")
                        if kind == "load":
                            pe.wait_ge(loaded, at(st["load"], i, LOADS, 16, 16))
                            for c in range(DC):
                                o = bank(u + c, i)
                                for k in range(NW):
                                    mm = pe.transpose(o[:, k * P:(k + 1) * P], x1tok[:, k, c * P:(c + 1) * P],
                                                      ident[:, :])
                                mm.then_inc(proj_full, 1)
                        elif kind == "rotate":
                            wait_taken(pe, st["load_use"] - 1, i)
                            wait_taken(pe, st["load_use"], i)
                            for co in range(DC):
                                o = bank(u + co, i)
                                for c in range(DC):
                                    mm = pe.matmul(o[:, :], rot[:, c, co * P:(co + 1) * P], x1T[:, c, :],
                                                   start=(c == 0), stop=(c == DC - 1))
                                mm.then_inc(proj_full, 1)
                        elif kind == "qkv":
                            if w == 0:
                                wait_taken(pe, st["x_use"] - 1, i)
                                wait_taken(pe, st["x_use"], i)
                            for k in range(3):
                                o = bank(u + k, i)
                                for c in range(DC):
                                    mm = pe.matmul(o[:, :], xs(s, c, w * P, P), wqkv[:, l, c, k * INNER:(k + 1) * INNER],
                                                   start=(c == 0), stop=(c == DC - 1))
                                mm.then_inc(proj_full, 1)
                        elif kind == "turn":
                            for k in range(2):
                                o = bank(u + k, i)
                                pe.wait_ge(rope_done, at(st["win"], i, WIN, 2, k + 1))
                                for c in range(IC):
                                    mm = pe.transpose(o[:, c * P:(c + 1) * P], roped[:, k, c * P:(c + 1) * P],
                                                      ident[:, :])
                                mm.then_inc(proj_full, 1)
                        elif kind == "score":
                            g = st["grp"]
                            wait(pe, exp_done, at(g, i, GRP, 1, -1))
                            if st["g"] == 0:
                                wait_taken(pe, st["turn_use"] - 1, i)
                                wait_taken(pe, st["turn_use"], i)
                            o = sc[g % 2]
                            n = 2 * P if w else P
                            pe.matmul(o[:, :, 0:n], ident_bf[:, :], mask[:, w % 2, :, 0:n], start=True, stop=False,
                                      skip_group_check=True)
                            for hh in range(2):
                                head = head_of(st["g"], hh)
                                r = slice(DH * (head % 2), DH * (head % 2) + DH)
                                mm = pe.matmul(o[:, hh, 0:n], qT[r, head // 2, :],
                                               kT[r, head // 2, :, :].rearrange("p a b -> p (a b)")[:, 0:n],
                                               start=False, stop=True, skip_group_check=True)
                            mm.then_inc(s_full, 1)
                        elif kind == "turn_p":
                            g = st["grp"]
                            pe.wait_ge(exp_done, at(g, i, GRP, 1, 1))
                            wait(pe, pt_taken[g % 2], at(g // 2, i, GRP // 2))
                            for hh in range(2):
                                for k in range(2 if w else 1):
                                    mm = pe.transpose(pt[g % 2][:, hh, k, :], prob[:, g % 4, hh, k * P:(k + 1) * P],
                                                      ident[:, :])
                            mm.then_inc(pt_full, 1)
                        elif kind == "pv":
                            g, win = st["grp"], st["win"]
                            pe.wait_ge(pt_taken[g % 2], at(g // 2, i, GRP // 2, 1, 1))
                            if st["g"] == 0:
                                wait(pe, o_ready, at(win, i, WIN))
                            for hh in range(2):
                                head = head_of(st["g"], hh)
                                slots = [(w % 2, win % 4)] + ([(1 - w % 2, (win - 1) % 4)] if w else [])
                                for k, (slot, v_at) in enumerate(slots):
                                    mm = pe.matmul(ob[:, head * DH:(head + 1) * DH], pT[:, g % 4, hh, slot, :],
                                                   vv[:, v_at, head * DH:(head + 1) * DH],
                                                   start=(k == 0), stop=(k == len(slots) - 1))
                            mm.then_inc(pv_done, 1)
                        elif kind == "turn_o":
                            pe.wait_ge(o_ready, at(st["win"], i, WIN, 1, 1))
                            o = bank(u, i)
                            for c in range(IC):
                                mm = pe.transpose(o[:, c * P:(c + 1) * P], on[:, c * P:(c + 1) * P], ident[:, :])
                            mm.then_inc(proj_full, 1)
                        elif kind == "wo":
                            wait_taken(pe, st["turn_o_use"], i)
                            o = bank(u, i)
                            for k in range(IC):
                                mm = pe.matmul(o[:, :], wo[:, l, k, st["c"] * P:(st["c"] + 1) * P], oT[:, k, :],
                                               start=(k == 0), stop=(k == IC - 1))
                            mm.then_inc(proj_full, 1)
                        elif kind == "mean":
                            wait_taken(pe, st["wo_use"], i)
                            o = bank(u, i)
                            for c in range(DC):
                                mm = pe.matmul(o[:, :], mean_w[:, :], xs(s, c), start=(c == 0), stop=(c == DC - 1))
                            mm.then_inc(proj_full, 1)
                        elif kind == "var":
                            pe.wait_ge(xsq_ready, at(st["ffn"], i, FFN, 1, 1))
                            o = bank(u, i)
                            for c in range(DC):
                                mm = pe.matmul(o[:, :], mean_w[:, :], xsq[:, c, :], start=(c == 0), stop=(c == DC - 1))
                            mm.then_inc(proj_full, 1)
                        elif kind in ("gate", "value"):
                            j = st["j"]
                            pe.wait_ge(h_ready, at(st["ffn"], i, FFN, DC, DC))
                            a = (HID if kind == "gate" else 0) + j * P
                            o = bank(u, i)
                            for c in range(DC):
                                mm = pe.matmul(o[0:HJ[j], :], w1[:, l, c, a:a + HJ[j]], h[:, c, :],
                                               start=(c == 0), stop=(c == DC - 1))
                            mm.then_inc(proj_full, 1)
                        elif kind == "down":
                            wait_taken(pe, st["value_use"], i)
                            o = bank(u, i)
                            for j in range(NJ):
                                mm = pe.matmul(o[:, :], w2[0:HJ[j], l, j, st["c"] * P:(st["c"] + 1) * P],
                                               hid[0:HJ[j], j, :], start=(j == 0), stop=(j == NJ - 1))
                            mm.then_inc(proj_full, 1)
                        elif kind == "out":
                            wait_taken(pe, st["x_use"] - 1, i)
                            wait_taken(pe, st["x_use"], i)
                            for k in range(2):
                                o = bank(u + k, i)
                                for t in range(2):
                                    for c in range(DC):
                                        mm = pe.transpose(o[:, t * D + c * P:t * D + (c + 1) * P],
                                                          xT[s][:, c, 1 + (2 * k + t) * P:1 + (2 * k + t + 1) * P],
                                                          ident[:, :])
                                mm.then_inc(proj_full, 1)
                    walk(pe, one)

                @block.scalar
                def _(a):
                    a.preload_act_table_set("natural_log_exp_and_others")

                    def one(st, i):
                        kind, s, u = st["kind"], st["s"], st["use"]
                        l, w = st.get("l"), st.get("w")
                        if kind in ("load", "rotate"):
                            for c in range(DC):
                                o = wait_full(a, u + c, i)
                                dst = x1T[:, c, :] if kind == "load" else xT[s][:, c, 1:T + 1]
                                a.copy(dst, o[:, :]).then_inc(proj_taken[(u + c) % NP], 1)
                        elif kind == "qkv":
                            wait(a, parts_ready, at(st["win"], i, WIN, 2, -2))
                            for k in range(3):
                                if k == 2:
                                    wait(a, pv_done, at(st["win"], i, WIN, 4, -8))
                                o = wait_full(a, u + k, i)
                                dst = raw[:, st["win"] % 2, k, :] if k < 2 else vv[:, st["win"] % 4, :]
                                a.copy(dst, o[:, :]).then_inc(proj_taken[(u + k) % NP], 1)
                        elif kind == "norm":
                            win = st["win"]
                            a.wait_ge(floored, at(win, i, WIN, 1, 1))
                            a.activation(lns[:, :], ss[:, :], ACT.Ln, scale=LN_SHIFT).then_inc(logged, 1)
                            a.wait_ge(logged, at(win, i, WIN, 1, 1))
                            a.activation(rn[:, :], lns[:, :], ACT.Exp, scale=-0.5, bias=consts[:, 1:2]
                                         ).then_inc(norm_ready, 1)
                        elif kind == "turn":
                            wait(a, s_full, at(st["win"], i, WIN, 4))
                            for k in range(2):
                                o = wait_full(a, u + k, i)
                                dst = kT[:, :, st["win"] % 2, :] if k else qT[:, :, :]
                                a.copy(dst, o[:, :].rearrange("p (c t) -> p c t", c=IC)
                                       ).then_inc(proj_taken[(u + k) % NP], 1)
                        elif kind == "score":
                            g = st["grp"]
                            n = 2 * P if w else P
                            a.wait_ge(max_done, at(g, i, GRP, 1, 1))
                            wait(a, pt_full, at(g, i, GRP, 1, -3))
                            for hh in range(2):
                                head = head_of(st["g"], hh)
                                ins = a.activation(prob[:, g % 4, hh, 0:n], sc[g % 2][:, hh, 0:n], ACT.Exp,
                                                   bias=nm[:, g % 4, hh:hh + 1],
                                                   accum_out=rs[:, st["win"] % 2, head:head + 1])
                            ins.then_inc(exp_done, 1)
                        elif kind == "turn_p":
                            if st["grp"] % 2:
                                move_p(a, a.copy, st, i)
                        elif kind == "turn_o":
                            o = wait_full(a, u, i)
                            a.copy(oT[:, :, w * P:(w + 1) * P], o[:, :].rearrange("p (c t) -> p c t", c=IC)
                                   ).then_inc(proj_taken[u % NP], 1)
                        elif kind == "mean":
                            wait_taken(a, u, i)
                            a.activation(xsq[:, :, :], xc[:, :, :], ACT.Square).then_inc(xsq_ready, 1)
                        elif kind == "var":
                            o = wait_full(a, u, i)
                            a.activation(lnv[:, :], o[:, :], ACT.Ln, bias=consts[:, 0:1]).then_inc(proj_taken[u % NP], 1)
                            wait_taken(a, u, i)
                            a.activation(rstd[:, :], lnv[:, :], ACT.Exp, scale=-0.5).then_inc(rstd_ready, 1)
                        elif kind == "gate":
                            j = st["j"]
                            o = wait_full(a, u, i)
                            a.activation(gb[0:HJ[j], j, :], o[0:HJ[j], :], ACT.Identity,
                                         bias=b1[0:HJ[j], l, 1, j:j + 1]).then_inc(proj_taken[u % NP], 1)
                        elif kind == "gelu":
                            wait_taken(a, st["gate_use"], i)
                            a.activation(gb[:, 0:NJ - 1, :], gb[:, 0:NJ - 1, :], ACT.Gelu)
                            a.activation(gb[0:HJ[-1], NJ - 1, :], gb[0:HJ[-1], NJ - 1, :], ACT.Gelu
                                         ).then_inc(gelu_done, 1)
                            a.preload_act_table_set("natural_log_exp_and_others")
                    walk(a, one)

                @block.gpsimd
                def _(pool):
                    for s in range(2):
                        ins = pool.memset(xT[s][:, :, 0:1], 0.0)
                    ins.then_inc(edge, 1)

                    def one(st, i):
                        kind = st["kind"]
                        if kind == "qkv":
                            for k in range(2):
                                wait_taken(pool, st["use"] + k, i)
                                if k == 0:
                                    wait(pool, summed, at(st["win"], i, WIN))
                                src = raw[:, st["win"] % 2, k, :]
                                pool.tensor_tensor(qksq[:, k * INNER:(k + 1) * INNER], src, src, ALU.mult
                                                   ).then_inc(squared, 1)
                        elif kind == "norm":
                            for k in range(2):
                                n = 2 * st["win"] + k
                                pool.wait_ge(parts_ready, at(n, i, 2 * WIN, 1, 1))
                                pool.tensor_tensor(direct[:, k, :], direct[:, k, :], swapped[:, k, :], ALU.add
                                                   ).then_inc(added, 1)
                                pool.wait_ge(added, at(n, i, 2 * WIN, 1, 1))
                                if k == 0:
                                    pool.wait_ge(norm_ready, at(st["win"], i, WIN, 1, 1))
                                pool.tensor_tensor(
                                    roped[:, k, :].rearrange("p (h d) -> p h d", h=H),
                                    direct[:, k, :].rearrange("p (h d) -> p h d", h=H),
                                    rn[:, k * H:(k + 1) * H].unsqueeze(2).to_broadcast([P, H, DH]), ALU.mult
                                ).then_inc(rope_done, 1)
                    walk(pool, one)

                @block.vector
                def _(v):
                    v.memset(outt[:, :, :], 0.0).then_inc(saved, 16)

                    def one(st, i):
                        kind, s, u = st["kind"], st["s"], st["use"]
                        l, w = st.get("l"), st.get("w")
                        if kind == "norm":
                            win = st["win"]
                            v.wait_ge(squared, at(win, i, WIN, 2, 2))
                            v.tensor_reduce(ss[:, :], qksq[:, :].rearrange("p (h d) -> p h d", h=2 * H), AX.X, ALU.add
                                            ).then_inc(summed, 1)
                            v.wait_ge(summed, at(win, i, WIN, 1, 1))
                            v.tensor_scalar(ss[:, :], ss[:, :], NORM_FLOOR, None, ALU.max).then_inc(floored, 1)
                            wait(v, added, at(win, i, WIN, 2))
                            for k in range(2):
                                src = raw[:, win % 2, k, :].rearrange("p (h d) -> p h d", h=H)
                                t = tabs[:, l, 2 * k, w, :].unsqueeze(1).to_broadcast([P, H, DH])
                                v.tensor_tensor(direct[:, k, :].rearrange("p (h d) -> p h d", h=H), src, t, ALU.mult)
                                sw = swapped[:, k, :].rearrange("p (h d) -> p h d", h=H)
                                for half in range(2):
                                    d0, s0 = half * DH // 2, (1 - half) * DH // 2
                                    t = tabs[:, l, 2 * k + 1, w, d0:d0 + DH // 2].unsqueeze(1).to_broadcast([P, H, DH // 2])
                                    ins = v.tensor_tensor(sw[:, :, d0:d0 + DH // 2], src[:, :, s0:s0 + DH // 2], t,
                                                          ALU.mult)
                                ins.then_inc(parts_ready, 1)
                        elif kind == "score":
                            g = st["grp"]
                            n = 2 * P if w else P
                            v.wait_ge(s_full, at(g, i, GRP, 1, 1))
                            v.tensor_reduce(nm[:, g % 4, :], sc[g % 2][:, :, 0:n], AX.X, ALU.max, negate=True
                                            ).then_inc(max_done, 1)
                        elif kind == "turn_p":
                            if st["grp"] % 2 == 0:
                                move_p(v, v.tensor_copy, st, i)
                        elif kind == "pv" and st["g"] == 3:
                            win = st["win"]
                            v.wait_ge(pv_done, at(win, i, WIN, 4, 4))
                            v.reciprocal(rr[:, :], rs[:, win % 2, :]).then_inc(inverted, 1)
                            v.wait_ge(inverted, at(win, i, WIN, 1, 1))
                            v.tensor_tensor(on[:, :].rearrange("p (h d) -> p h d", h=H),
                                            ob[:, :].rearrange("p (h d) -> p h d", h=H),
                                            rr[:, :].unsqueeze(2).to_broadcast([P, H, DH]), ALU.mult
                                            ).then_inc(o_ready, 1)
                        elif kind == "wo":
                            o = wait_full(v, u, i)
                            x_ = xT[s][:, st["c"], 1:T + 1]
                            v.tensor_tensor(x_, o[:, :], x_, ALU.add).then_inc(proj_taken[u % NP], 1)
                        elif kind == "mean":
                            o = wait_full(v, u, i)
                            for c in range(DC):
                                ins = v.tensor_tensor(xc[:, c, :], xs(s, c), o[:, :], ALU.subtract)
                            ins.then_inc(proj_taken[u % NP], 1)
                        elif kind == "hnorm":
                            v.wait_ge(rstd_ready, at(st["ffn"], i, FFN, 1, 1))
                            for c in range(DC):
                                v.scalar_tensor_tensor(h[:, c, :], xc[:, c, :], lng[:, l, c:c + 1], rstd[:, :],
                                                       ALU.mult, ALU.mult).then_inc(h_ready, 1)
                        elif kind == "value":
                            j = st["j"]
                            if j == 0:
                                v.wait_ge(gelu_done, at(st["ffn"], i, FFN, 1, 1))
                            o = wait_full(v, u, i)
                            v.scalar_tensor_tensor(hid[0:HJ[j], j, :], o[0:HJ[j], :], b1[0:HJ[j], l, 0, j:j + 1],
                                                   gb[0:HJ[j], j, :], ALU.add, ALU.mult).then_inc(proj_taken[u % NP], 1)
                        elif kind == "down":
                            o = wait_full(v, u, i)
                            x_ = xT[s][:, st["c"], 1:T + 1]
                            v.scalar_tensor_tensor(x_, o[:, :], b2[:, l, st["c"]:st["c"] + 1], x_, ALU.add, ALU.add
                                                   ).then_inc(proj_taken[u % NP], 1)
                        elif kind == "out":
                            v.wait_ge(saved, at(st["outs"], i, OUTS, 16, 16))
                            v.wait_ge(reloaded, at(st["outs"], i, OUTS, 16, 16))
                            for k in range(2):
                                o = wait_full(v, u + k, i)
                                v.tensor_tensor(outt[:, 2 * k:2 * k + 2, :], o[:, :].rearrange("p (t d) -> p t d", t=2),
                                                x1out[:, 2 * k:2 * k + 2, :], ALU.add
                                                ).then_inc(proj_taken[(u + k) % NP], 1)
                    walk(v, one)


def rotary_tables():
    f = np.float32
    half = np.arange(0, DH, 2, dtype=f)
    inv_freq = (f(1.0) / np.power(f(10000.0), half / f(DH))).astype(f)
    t = np.arange(T, dtype=f)
    freqs = t[:, None] * inv_freq[None, :]
    freqs = np.concatenate([freqs, freqs], axis=-1)
    base = ((half + f(0.4 * DH)) / f(1.4 * DH)).astype(f)
    power = ((t - f(T // 2)) / f(64.0)).astype(f)
    scale = np.power(base[None, :], power[:, None]).astype(f)
    scale = np.concatenate([scale, scale], axis=-1)
    cos, sin = np.cos(freqs), np.sin(freqs)
    sign = np.where(np.arange(DH) < DH // 2, f(-1.0), f(1.0))[None, :]
    return np.ascontiguousarray(np.stack([f(8.0) * cos * scale, f(8.0) * sin * scale * sign,
                                          cos / scale, sin / scale * sign]).astype(f))


_INS = ["x", "cond_256", "cond_64", "L0_cond_input_basis", "L0_cond_mode_to_rank", "L0_cond_output_basis",
        "L0_ffn_router_w", "L0_ffn_w1", "L0_ffn_w2", "L1_cond_q_right", "L1_cond_spectral_gate",
        "L1_ffn_wqkv", "L1_ffn_q_scale", "L1_ffn_k_scale", "L1_ffn_wo", "L1_ffn_ln_g", "L1_ffn_ln_b",
        "L1_ffn_w1", "L1_ffn_b1", "L1_ffn_w2", "L1_ffn_b2"]


def kernel(**inputs):
    import numpy as _np
    import concourse.bacc as _bacc
    from concourse import mybir as _mybir
    from concourse.bass_utils import run_bass_kernel_spmd as _run

    nc = _bacc.Bacc("TRN2", target_bir_lowering=False, num_devices=1)
    arrays, args = {}, []
    for name in _INS + ["rotary"]:
        a = rotary_tables() if name == "rotary" else _np.ascontiguousarray(inputs[name])
        arrays[f"in_{name}_dram"] = a
        args.append(nc.dram_tensor(f"in_{name}_dram", a.shape, _mybir.dt.from_np(a.dtype), kind="ExternalInput").ap())
    args.append(nc.dram_tensor("out_0_dram", (B, T, D), F32, kind="ExternalOutput").ap())
    build(nc, *args)
    r = _run(nc, [arrays], core_ids=[0])
    return r.results[0]["out_0_dram"]
```

```python
from contextlib import ExitStack

import concourse.bass as bass
from concourse import mybir
from concourse.alu_op_type import AluOpType as ALU
import numpy as np

F32 = mybir.dt.float32
BF16 = mybir.dt.bfloat16
U32 = mybir.dt.uint32
ACT = mybir.ActivationFunctionType
AX = mybir.AxisListType

P = 128
B, T, D = 8, 512, 256
DC = D // P
NW = T // P
K = 64
E, F = 8, 512
FC = F // P
TOP = 2
G = TOP * NW
XW = D + 1
REGION = B * T + P
TILES = TOP * B * T // P + E
SPARE = E
SLOTS = E * REGION + SPARE * P
N_MADE = 19
L = 2
H, DH = 8, 64
INNER = H * DH
IC = INNER // P
HID = D * 4 * 2 // 3
HJ = [P] * ((HID - P // 2) // P) + [(HID - P // 2) % P, P // 2]
NJ = len(HJ)
AT = [sum(HJ[:j]) for j in range(NJ)]
FULL = NJ - 2
GATE_AT = [HID + HJ[-1] + AT[j] for j in range(NJ - 1)] + [HID]
MASKED = -1.0e30
LN_EPS = 1e-5
NORM_FLOOR = 1e-24
LN_SHIFT = 2.0 ** 20



class Counter:
    def __init__(self, start=None):
        self.n = dict(start or {})

    def take(self, name, k):
        v = self.n.get(name, 0)
        self.n[name] = v + k
        return v


def window_start(s, l, w):
    return [dict(kind=kind, s=s, l=l, w=w) for kind in ("qkv", "rope", "norm", "turn")]


WINDOW_ORDER = """
    score:0 score:1 qkv rope turn_p:0 score:2 turn_p:1 norm
    score:3 pv:0 turn_o pv:1 turn_p:2 turn_p:3 turn pv:2 pv:3
""".split()


def attention_steps(s, l, after):
    out = []
    for w in range(NW):
        following = window_start(s, l, w + 1) if w + 1 < NW else window_start(*after, 0) if after else []
        following = {x["kind"]: x for x in following}
        for name in WINDOW_ORDER:
            kind, _, g = name.partition(":")
            if g:
                out.append(dict(kind=kind, s=s, l=l, w=w, g=int(g)))
            elif kind == "turn_o":
                if w:
                    out.append(dict(kind=kind, s=s, l=l, w=w - 1))
            elif kind in following:
                out.append(following[kind])
    return out


def ffn_steps(s, l):
    def st(kind, **kw):
        return dict(kind=kind, s=s, l=l, **kw)
    room = [None]
    out = [st("turn_o", w=NW - 1)] + room + [st("wo", c=c) for c in range(DC)] + room + [st("mean")] + room
    out += [st("var"), st("hnorm")] + room + [st("gate", j=j) for j in range(NJ)] + [st("gelu")]
    out += [st("value", j=j) for j in range(NJ - 1)] + [st("down", c=c) for c in range(DC)]
    return out


def load_steps(s):
    return [dict(kind="load", s=s), dict(kind="rotate", s=s)]


def pick_steps(s):
    return [dict(kind="pick", s=s, k=k) for k in range(TOP)]


def out_steps(s):
    return [dict(kind="out", s=s)]


def weight(step):
    weight = {"qkv": 1.2}.get(step["kind"], 1.0)
    return weight * (1.4 if step["w"] == 0 and step["kind"] in ("score", "turn_p", "pv") else 1.0)


def merge(attention, other, upto):
    out, j, gone = [], 0, 0.0
    total = sum(weight(x) for x in attention[:upto])
    for i, x in enumerate(attention):
        out.append(x)
        gone += weight(x)
        while j < len(other) and (i + 1 >= upto or (j + 1) * total <= gone * len(other) + 1e-9):
            if other[j]:
                out.append(other[j])
            j += 1
    assert j == len(other)
    return out


def before_next(attention):
    return max(i for i, x in enumerate(attention) if x["kind"] == "qkv")


def head_of(g, hh):
    return 4 * (g // 2) + g % 2 + 2 * hh


USES = dict(qkv=3, turn=2, turn_o=1, wo=1, mean=1, var=1, gate=1, value=1, down=1, load=DC, rotate=DC, out=NW)


def number(steps, c):
    out = []
    for st in steps:
        st = dict(st)
        kind, s = st["kind"], st["s"]
        st["use"] = c.take("use", USES.get(kind, 0))
        if kind in ("qkv", "rope", "norm", "turn", "turn_o"):
            st["win"] = c.take("win_" + kind, 1)
        if kind in ("score", "turn_p", "pv"):
            st["grp"] = c.take("grp_" + kind, 1)
            st["win"] = st["grp"] // 4
        st["ffn"] = c.take("ffn", kind == "down" and st["c"] == DC - 1)
        st["load"] = c.take("load", kind == "load")
        st["pick"] = c.take("pick", kind == "pick" and st["k"] == TOP - 1)
        st["outs"] = c.take("outs", kind == "out")
        for what in ("qkv", "turn", "turn_o", "wo", "gate", "value", "load"):
            st[what + "_use"] = c.n.get("last_" + what)
        st["x_use"] = c.n.get(f"last_x{s}")
        if kind in USES:
            c.n["last_" + kind] = st["use"] + USES[kind] - 1
        if kind in ("rotate", "down"):
            c.n[f"last_x{s}"] = c.n["last_" + kind]
        out.append(st)
    return out


def schedule():
    def section(att, after, other):
        steps = attention_steps(*att, after)
        return merge(steps, other, before_next(steps) if after else len(steps) - 1)

    c = Counter()
    first = number(pick_steps(0) + load_steps(0) + window_start(0, 0, 0)
                   + section((0, 0), (1, 0), pick_steps(1) + load_steps(1)), c)
    start = dict(c.n)
    def front(picks):
        return section((1, 0), (0, 1), ffn_steps(0, 0)) + section((0, 1), (1, 1), ffn_steps(1, 0) + picks)
    third = section((1, 1), (0, 0), ffn_steps(0, 1) + out_steps(0) + load_steps(0))
    fourth = section((0, 0), (1, 0), pick_steps(1) + ffn_steps(1, 1) + out_steps(1) + load_steps(1))
    body = number(front(pick_steps(0)) + third + fourth, c)
    per = {k: c.n[k] - start.get(k, 0) for k in c.n if not k.startswith("last_")}
    for what in ("turn", "turn_o"):
        assert c.n["last_" + what] - start["last_" + what] == per["use"]
    last = number(front([]) + section((1, 1), None, ffn_steps(0, 1) + out_steps(0))
                  + [x for x in ffn_steps(1, 1) if x] + out_steps(1), Counter(start))
    return first, body, last, per


def build(nc, x, cond_256, cond_64, L0_cond_input_basis, L0_cond_mode_to_rank, L0_cond_output_basis,
          L0_ffn_router_w, L0_ffn_w1, L0_ffn_w2, L1_cond_q_right, L1_cond_spectral_gate,
          L1_ffn_wqkv, L1_ffn_q_scale, L1_ffn_k_scale, L1_ffn_wo, L1_ffn_ln_g, L1_ffn_ln_b,
          L1_ffn_w1, L1_ffn_b1, L1_ffn_w2, L1_ffn_b2, rotary, out):
    first, body, last, per = schedule()
    NP = 3
    USE, WIN, GRP, FFN, OUTS = per["use"], per["win_qkv"], per["grp_pv"], per["ffn"], per["outs"]
    LOADS = per["load"]
    assert per["pick"] == LOADS
    assert USE % NP == 0 and WIN % 4 == 0 and GRP % 4 == 0
    ITER = B // 2
    slots_x = nc.dram_tensor("slots_x", [SLOTS, XW], F32, kind="Internal").ap()
    slots_y = nc.dram_tensor("slots_y", [TILES * P, D], F32, kind="Internal").ap()
    SY = slots_y.rearrange("(t p) d -> t p d", p=P)
    x1 = nc.dram_tensor("x_after_moe", [B, P, NW, D], F32, kind="Internal").ap()

    with ExitStack() as whole:
        def scope(stack):
            return (lambda name, shape, dt=F32: stack.enter_context(nc.sbuf_tensor(name, shape, dt)),
                    lambda name, shape, dt=F32: stack.enter_context(nc.psum_tensor(name, shape, dt)),
                    lambda name: stack.enter_context(nc.semaphore(name)))

        sb, _, sem = scope(whole)
        ident = sb("ident", [P, P])
        mean_w = sb("mean_w", [P, P])
        ident_bf = sb("ident_bf", [P, P], BF16)
        mask = sb("mask", [P, 2, 2, 2 * P], BF16)
        tabs = sb("tabs", [P, L, 4, NW, DH])
        rot = sb("rot", [P, DC, D])
        wqkv = sb("wqkv", [P, L, DC, 3 * INNER])
        wo = sb("wo", [P, L, IC, D])
        w1 = sb("w1", [P, L, DC, 2 * HID])
        w2 = sb("w2", [P, L, NJ, D])
        lng = sb("lng", [P, L, DC])
        b1 = sb("b1", [P, L, 2, NJ])
        b2 = sb("b2", [P, L, DC])
        consts = sb("consts", [P, 4])
        y_row = sb("y_row", [P, B, G], U32)
        layer_weights = sem("layer_weights")

        expert_w = sem("expert_w")
        x1tok = sb("x1tok", [P, NW, D])
        loaded = sem("loaded")
        small_b = sem("small_b")
        XROW = x.rearrange("b (w p) d -> b p w d", p=P)

        experts = ExitStack()
        sb_e = lambda name, shape, dt=F32: experts.enter_context(nc.sbuf_tensor(name, shape, dt))
        w1m = sb_e("w1m", [P, E, DC, F])
        w2m = sb_e("w2m", [P, E, FC, D])
        tile_row = sb_e("tile_row", [1, TILES], U32)
        tile_expert = sb_e("tile_expert", [1, TILES], U32)

        with ExitStack() as st:
            sb, ps, sem = scope(st)
            rw = sb("rw", [P, DC, E])
            lnb = sb("lnb", [P, L, DC])
            b1raw = sb("b1raw", [P, L, 2, NJ])
            basis = sb("basis", [K, D])
            basisT = sb("basisT", [P, DC, K])
            raw = sb("raw", [K, K])
            rawT = sb("rawT", [K, K])
            outb = sb("outb", [K, D + E])
            outbT = sb("outbT", [P, DC, K])
            c256 = sb("c256", [P, B])
            c64 = sb("c64", [K, B])
            aug = sb("aug", [K, 2 * K])
            row = sb("row", [K, 2 * K])
            below = sb("below", [K, K])
            small = sb("small", [K, 16])
            UT = sb("UT", [K, K])
            mtr = sb("mtr", [K, P])
            pace = sb("pace", [P, 10])
            prod = sb("prod", [K, K])
            srow = sb("srow", [K, 1])
            qr = sb("qr", [P, 4])
            nql = sb("nql", [P, 4])
            nqr = sb("nqr", [P, 4])
            ql = sb("ql", [P, 4])
            gate = sb("gate", [P, 1])
            ss = sb("ss", [P, 8])
            sq8 = sb("sq8", [P, 2, B])
            Lm = sb("Lm", [P, 4, 4])
            Rm = sb("Rm", [P, 4, 4])
            coef = sb("coef", [P, 4, 4])
            cterm = sb("cterm", [P, 4, 4])
            rtab = sb("rtab", [P, 4, NW, DH])
            sc = sb("sc", [P, L, 4, DH])
            iota_i = sb("iota_i", [P, E + 1], mybir.dt.int32)
            region_i = sb("region_i", [P, E + 1], mybir.dt.int32)
            lim_i = sb("lim_i", [P, T * B // P], mybir.dt.int32)
            off_i = sb("off_i", [P, TILES], mybir.dt.int32)
            iota8 = sb("iota8", [P, E + 1])
            region = sb("region", [P, E + 1])
            limit = sb("limit", [P, T * B // P])
            offset = sb("offset", [P, TILES])
            earlier = sb("earlier", [P, P], BF16)
            ones = sb("ones", [P, P])
            ones_bf = sb("ones_bf", [P, P], BF16)
            zero = sb("zero", [P, XW])
            xin = [sb(f"xin{i}", [P, NW, D]) for i in range(2)]
            xT = sb("xTa", [P, DC, T])
            projT = sb("projT", [K, T])
            hidT = sb("hidT", [K, T])
            xo = [sb(f"xo{i}", [P, 2, NW, XW]) for i in range(2)]
            lg = sb("lg", [P, NW, E])
            m8 = sb("m8", [P, NW, 8])
            i8 = sb("i8", [P, NW, 8], U32)
            i8f = sb("i8f", [P, NW, 2])
            gap = sb("gap", [P, NW])
            eg = sb("eg", [P, NW])
            den = sb("den", [P, NW])
            hits = sb("hits", [P, B + 1, G, E], BF16)
            hit_sum = sb("hit_sum", [P, E])
            hits_before = sb("hits_before", [P, E], BF16)
            cand = sb("cand", [P, G, E])
            cand_all = sb("cand_all", [P, B * G, E])
            shifts = sb("shifts", [P, B * G])
            slot_now = sb("slot_now", [P, G])
            slot = sb("slot", [P, B + 1, G])
            idx = [sb(f"idx{i}", [P, G], U32) for i in range(2)]
            spare_idx = sb("spare_idx", [P, SPARE], U32)
            pad_start = sb("pad_start", [1, E], U32)
            count = sb("count", [P, E])
            over = sb("over", [P, E, T * B // P])
            tiles = sb("tiles", [P, E + 1])
            end = sb("end", [P, E + 1])
            begin = sb("begin", [P, E + 1])
            shift = sb("shift", [P, E + 1])
            tile_a = sb("tile_a", [1, TILES, E + 1])
            tile_b = sb("tile_b", [1, TILES, E + 1])
            tile_f = sb("tile_f", [1, TILES])

            xb = ps("xb", [P, NW, 512])
            tb = [ps(f"tb{i}", [P, 512]) for i in range(2)]
            pb = ps("pb", [P, 512])
            rk = ps("rk", [P, 512])
            lnb_b = xb[:, 0, :]

            basis_in = sem("basis_in")
            ffn_w1_in = sem("ffn_w1_in")
            small_in = sem("small_in")
            made = sem("made")
            pe_prep = sem("pe_prep")
            v_prep = sem("v_prep")
            p_prep = sem("p_prep")
            a_prep = sem("a_prep")
            x_in = [sem(f"x_in{i}") for i in range(2)]
            x_full = sem("x_full")
            x_copied = sem("x_copied")
            proj_full = sem("proj_full_r")
            projT_done = sem("projT_done")
            hid_full = sem("hid_full")
            hidT_done = sem("hidT_done")
            hits_ready = sem("hits_ready")
            rank_full = sem("rank_full")
            xo_full = sem("xo_full")
            xo_copied = sem("xo_copied")
            lg_taken = sem("lg_taken")
            slot_ready = sem("slot_ready")
            scattered = [sem(f"scattered{i}") for i in range(2)]
            passed = sem("passed")
            totals = sem("totals")
            pads_ready = sem("pads_ready")
            padded = sem("padded")
            lnb_full = sem("lnb_full")
            chain = sem("chain")
            exp_done = sem("exp_done_a")
            gap_done = sem("gap_done")

            N_SMALL = 24
            PREP_QN = 5

            with nc.Block() as block:
                @block.sync
                def _(sp):
                    n = [0]

                    def small_load(dst, src, eng=sp):
                        eng.dma_start(dst, src, allow_slow_non_contiguous=True).then_inc(small_in, 16)
                        n[0] += 1
                    sp.dma_start(raw[:, :], L0_cond_mode_to_rank).then_inc(basis_in, 16)
                    sp.dma_start(basis[:, :], L0_cond_input_basis).then_inc(basis_in, 16)
                    sp.dma_start(outb[:, 0:D], L0_cond_output_basis).then_inc(basis_in, 16)
                    for half in range(2):
                        small_load(c256[half * K:(half + 1) * K, :], cond_256.rearrange("b k -> k b"))
                        small_load(qr[half * K:(half + 1) * K, :], L1_cond_q_right.rearrange("q k -> k q"))
                        small_load(gate[half * K:(half + 1) * K, :],
                                   L1_cond_spectral_gate.rearrange("a b c k -> k (a b c)"))
                    small_load(c64[:, :], cond_64.rearrange("b k -> k b"))
                    small_load(rw[:, :, :], L0_ffn_router_w.rearrange("(c p) e -> p c e", p=P))
                    small_load(rtab[:, :, :, :], rotary.rearrange("k (w p) d -> p k w d", p=P))
                    for l in range(L):
                        for kind, src in ((0, L1_ffn_q_scale), (2, L1_ffn_k_scale)):
                            small_load(sc[:, l, kind, :], src[l].partition_broadcast(P))
                            small_load(sc[:, l, kind + 1, 0:DH // 2],
                                       src[l, DH // 2:DH].partition_broadcast(P))
                            small_load(sc[:, l, kind + 1, DH // 2:DH],
                                       src[l, 0:DH // 2].partition_broadcast(P))
                    small_load(lng[:, :, :], L1_ffn_ln_g.rearrange("l (c p) -> p l c", p=P))
                    small_load(lnb[:, :, :], L1_ffn_ln_b.rearrange("l (c p) -> p l c", p=P))
                    small_load(b2[:, :, :], L1_ffn_b2.rearrange("l (c p) -> p l c", p=P))
                    assert n[0] == N_SMALL, n[0]
                    for par in range(2):
                        sp.dma_start(xin[par][:, :, :], XROW[par]).then_inc(x_in[par], 16)
                    for l in range(L):
                        src = L1_ffn_w1[l].rearrange("(c p) n -> p c n", p=P)
                        for to, at_, n_ in ((0, 0, HID), (HID, HID + AT[-1], HJ[-1]), (HID + HJ[-1], HID, AT[-1])):
                            sp.dma_start(w1[:, l, :, to:to + n_], src[:, :, at_:at_ + n_]).then_inc(ffn_w1_in, 16)
                    for e in range(E):
                        sp.dma_start(w1m[:, e, :, :], L0_ffn_w1[e].rearrange("(c p) f -> p c f", p=P)
                                     ).then_inc(expert_w, 16)
                        sp.dma_start(w2m[:, e, :, :], L0_ffn_w2[e].rearrange("(c p) d -> p c d", p=P)
                                     ).then_inc(expert_w, 16)
                    for l in range(L):
                        sp.dma_start(wqkv[:, l, :, :], L1_ffn_wqkv[l].rearrange("(c p) n -> p c n", p=P)
                                     ).then_inc(layer_weights, 16)
                        sp.dma_start(wo[:, l, :, :], L1_ffn_wo[l].rearrange("(c p) n -> p c n", p=P)
                                     ).then_inc(layer_weights, 16)
                        sp.dma_start(w2[:, l, 0:FULL, :], L1_ffn_w2[l, 0:FULL * P].rearrange("(j p) n -> p j n", p=P)
                                     ).then_inc(layer_weights, 16)
                        for j in range(FULL, NJ):
                            sp.dma_start(w2[0:HJ[j], l, j, :], L1_ffn_w2[l, AT[j]:AT[j] + HJ[j]]
                                         ).then_inc(layer_weights, 16)
                    with sp.Fori(0, B // 2 - 1) as i:
                        for par in range(2):
                            sp.wait_ge(x_full, i * 2 * DC + (par + 1) * DC)
                            sp.dma_start(xin[par][:, :, :], XROW[i * 2 + (par + 2)]).then_inc(x_in[par], 16)
                    sp.wait_ge(pads_ready, 1)
                    for e in range(E):
                        first_row = sp.value_load(pad_start[0:1, e:e + 1], min_val=0, max_val=SLOTS - P)
                        sp.dma_start(slots_x[bass.ds(first_row, P), :], zero[:, :]).then_inc(padded, 16)
                    sp.wait_ge(padded, 16 * E)
                    sp.wait_ge(layer_weights, 16 * 5 * L)

                @block.gpsimd
                def _(pool):
                    pool.memset(ident[:, :], 0.0).then_inc(made, 1)
                    pool.memset(ones[:, :], 1.0).then_inc(made, 1)
                    pool.memset(below[:, :], 0.0).then_inc(made, 1)
                    pool.memset(mask[:, :, :, :], 0.0).then_inc(made, 1)
                    pool.memset(earlier[:, :], 1.0).then_inc(made, 1)
                    pool.memset(ones_bf[:, :], 1.0).then_inc(made, 1)
                    pool.memset(zero[:, :], 0.0).then_inc(made, 1)
                    pool.iota(iota_i[:, :], [[1, E + 1]], base=0, channel_multiplier=0).then_inc(made, 1)
                    pool.iota(region_i[:, :], [[REGION, E + 1]], base=0, channel_multiplier=0).then_inc(made, 1)
                    pool.iota(lim_i[:, :], [[P, T * B // P]], base=0, channel_multiplier=0).then_inc(made, 1)
                    pool.iota(off_i[:, :], [[P, TILES]], base=0, channel_multiplier=0).then_inc(made, 1)
                    pool.iota(spare_idx[:, :], [[P, SPARE]], base=E * REGION, channel_multiplier=1).then_inc(made, 1)
                    pool.wait_ge(made, 12)
                    pool.affine_select(out=earlier[:, :], in_=earlier[:, :], compare_op=ALU.is_gt, fill=0.0,
                                       base=0, pattern=[[1, P]], channel_multiplier=-1).then_inc(made, 1)
                    pool.affine_select(out=ident[:, :], in_=ident[:, :], compare_op=ALU.not_equal, fill=1.0,
                                       base=0, pattern=[[-1, P]], channel_multiplier=1).then_inc(made, 1)
                    pool.affine_select(out=below[:, :], in_=below[:, :], compare_op=ALU.is_ge, fill=-1.0,
                                       base=0, pattern=[[1, K]], channel_multiplier=-1).then_inc(made, 1)
                    for par in range(2):
                        cur = mask[:, par, :, par * P:(par + 1) * P]
                        prev = mask[:, par, :, (1 - par) * P:(2 - par) * P]
                        pool.affine_select(out=cur, in_=cur, compare_op=ALU.is_ge, fill=MASKED, base=0,
                                           pattern=[[0, 2], [-1, P]], channel_multiplier=1).then_inc(made, 1)
                        pool.affine_select(out=prev, in_=prev, compare_op=ALU.is_ge, fill=MASKED, base=0,
                                           pattern=[[0, 2], [1, P]], channel_multiplier=-1).then_inc(made, 1)

                    def scatter(n, par):
                        pool.wait_ge(slot_ready, n + 2)
                        pool.wait_ge(xo_copied, n + 2)
                        pool.wait_ge(passed, n + 1)
                        pool.tensor_tensor(pace[:, 8:9], pace[:, 6:7], pace[:, 7:8], ALU.add).then_inc(passed, 1)
                        for k in range(2):
                            for w in range(NW):
                                g = k * NW + w
                                pool.indirect_dma_start(
                                    out=slots_x, out_offset=bass.IndirectOffsetOnAxis(ap=idx[par][:, g:g + 1], axis=0),
                                    in_=xo[par][:, k, w, :], in_offset=None).then_inc(scattered[par], 16)
                    n = [0]

                    def pool_step(ins):
                        n[0] += 1
                        ins.then_inc(p_prep, 1)
                        pool.wait_ge(p_prep, n[0])
                    pool.wait_ge(small_in, 16 * N_SMALL)
                    pool.wait_ge(made, N_MADE)
                    pool.tensor_scalar(mean_w[:, :], ones[:, :], 1.0 / D, None, ALU.mult)
                    pool.tensor_copy(ident_bf[:, :], ident[:, :])
                    for k, val in enumerate((LN_EPS, 10 * float(np.log(2.0)), 1e-8, 0.0)):
                        pool.memset(consts[:, k:k + 1], val)
                    pool.tensor_tensor(sq8[:, 0, :], c256[:, :], c256[:, :], ALU.mult)
                    pool.memset(sq8[:, 1, 4:8], 0.0)
                    pool_step(pool.tensor_tensor(sq8[:, 1, 0:4], qr[:, :], qr[:, :], ALU.mult))
                    for n_ in (4, 2):
                        pool_step(pool.tensor_tensor(sq8[:, :, 0:n_], sq8[:, :, 0:n_], sq8[:, :, n_:2 * n_], ALU.add))
                    pool_step(pool.tensor_tensor(ss[:, 0:2], sq8[:, :, 0], sq8[:, :, 1], ALU.add))
                    pool_step(pool.tensor_scalar(ss[:, 0:2], ss[:, 0:2], 1e-8, None, ALU.add))
                    QN = n[0]
                    pool.wait_ge(a_prep, 2)
                    pool_step(pool.tensor_tensor(ss[:, 4:6], ss[:, 2:4], ss[:, 2:4], ALU.mult))
                    pool_step(pool.tensor_tensor(ss[:, 4:6], ss[:, 4:6], ss[:, 0:2], ALU.mult))
                    pool_step(pool.tensor_scalar(ss[:, 4:6], ss[:, 4:6], -0.5, 1.5, ALU.mult, ALU.add))
                    pool_step(pool.tensor_tensor(ss[:, 6:8], ss[:, 4:6], ss[:, 2:4], ALU.mult))
                    pool_step(pool.tensor_scalar(ql[:, :], c256[:, 0:4], ss[:, 6:7], None, ALU.mult))
                    pool_step(pool.tensor_scalar(qr[:, :], qr[:, :], ss[:, 7:8], gate[:, 0:1], ALU.mult, ALU.mult))
                    pool_step(pool.tensor_scalar(nql[:, :], ql[:, :], -1.0, None, ALU.mult))
                    pool_step(pool.tensor_scalar(nqr[:, :], qr[:, :], -1.0, None, ALU.mult))
                    W_, X_, Y_, Z_ = 0, 1, 2, 3
                    left = [[(1, W_), (-1, X_), (-1, Y_), (-1, Z_)], [(1, X_), (1, W_), (-1, Z_), (1, Y_)],
                            [(1, Y_), (1, Z_), (1, W_), (-1, X_)], [(1, Z_), (-1, Y_), (1, X_), (1, W_)]]
                    right = [[(1, W_), (-1, X_), (-1, Y_), (-1, Z_)], [(1, X_), (1, W_), (1, Z_), (-1, Y_)],
                             [(1, Y_), (-1, Z_), (1, W_), (1, X_)], [(1, Z_), (1, Y_), (-1, X_), (1, W_)]]
                    for o in range(4):
                        for m in range(4):
                            s_, q_ = left[o][m]
                            pool.tensor_copy(Lm[:, m, o:o + 1], (ql if s_ > 0 else nql)[:, q_:q_ + 1])
                            s_, q_ = right[o][m]
                            s_ = s_ if q_ == W_ else -s_
                            last = pool.tensor_copy(Rm[:, o, m:m + 1], (qr if s_ > 0 else nqr)[:, q_:q_ + 1])
                    pool_step(last)
                    for m in range(4):
                        dst = coef if m == 0 else cterm
                        pool_step(pool.tensor_tensor(dst[:, :, :], Lm[:, m, :].unsqueeze(2).to_broadcast([P, 4, 4]),
                                             Rm[:, m, :].unsqueeze(1).to_broadcast([P, 4, 4]), ALU.mult))
                        if m:
                            pool_step(pool.tensor_tensor(coef[:, :, :], coef[:, :, :], cterm[:, :, :], ALU.add))
                    for half in range(2):
                        p0 = half * K
                        for c in range(DC):
                            for o in range(4):
                                last = pool.tensor_scalar(
                                    rot[p0:p0 + K, c, o * K:(o + 1) * K], ident[p0:p0 + K, p0:p0 + K],
                                    coef[p0:p0 + K, o, 2 * c + half:2 * c + half + 1], None, ALU.mult)
                        pool_step(last)
                    for l in range(L):
                        for kind in range(4):
                            last = pool.tensor_tensor(tabs[:, l, kind, :, :], rtab[:, kind, :, :],
                                                   sc[:, l, kind, :].unsqueeze(1).to_broadcast([P, NW, DH]), ALU.mult)
                    pool_step(last)
                    assert QN == PREP_QN, QN
                    for n in range(SPARE):
                        pool.indirect_dma_start(
                            out=slots_x, out_offset=bass.IndirectOffsetOnAxis(ap=spare_idx[:, n:n + 1], axis=0),
                            in_=zero[:, :], in_offset=None).then_inc(scattered[n % 2], 16)
                    pool.wait_ge(v_prep, 3)
                    with pool.Fori(0, B // 2) as i:
                        for par in range(2):
                            scatter(i * 2 + par, par)
                    for s in scattered:
                        pool.wait_ge(s, 16 * G * (B // 2) + 16 * SPARE // 2)

                @block.tensor
                def _(pe):
                    pe.wait_ge(basis_in, 16 * 3)
                    pe.wait_ge(made, N_MADE)
                    n = [0]

                    def done(mm):
                        n[0] += 1
                        mm.then_inc(pe_prep, 1)
                    done(pe.matmul(rk[0:K, 0:K], raw[:, :], raw[:, :], start=True, stop=True))
                    done(pe.transpose(pb[0:K, 0:K], raw[:, :], ident[0:K, 0:K]))
                    for c in range(DC):
                        pe.transpose(tb[0][:, c * K:(c + 1) * K], outb[:, c * P:(c + 1) * P], ident[0:K, 0:K])
                    for c in range(DC):
                        mm = pe.transpose(tb[1][:, c * K:(c + 1) * K], basis[:, c * P:(c + 1) * P], ident[0:K, 0:K])
                    done(mm)
                    assert n[0] == 3
                    def turn_x(par, n):
                        pe.wait_ge(x_in[par], n * 16 + 16)
                        for c in range(DC):
                            for w in range(NW):
                                mm = pe.transpose(tb[c][:, w * P:(w + 1) * P], xin[par][:, w, c * P:(c + 1) * P],
                                                  ident[:, :])
                            mm.then_inc(x_full, 1)

                    shifts_of = [(l, side, j) for l in range(L) for side in range(2) for j in range(NJ)]

                    def shift_product(l, side, j):
                        col, f = (l * 2 + side) * NJ + j, (GATE_AT if side else AT)[j]
                        for c in range(DC):
                            mm = pe.matmul(lnb_b[0:HJ[j], col:col + 1], w1[:, l, c, f:f + HJ[j]],
                                           lnb[:, l, c:c + 1], start=(c == 0), stop=(c == DC - 1))
                        return mm
                    for k in range(K):
                        pe.wait_ge(v_prep, 3 + 3 * k)
                        pe.matmul(rk[0:K, k:K + k + 1], ident[0:K, k:k + 1].to_broadcast([K, K]), aug[:, k:K + k + 1],
                                  start=True, stop=True).then_inc(pe_prep, 1)
                        if k == K // 4:
                            turn_x(0, 0)
                        if k == K // 2 - 1:
                            pe.wait_ge(small_in, 16 * N_SMALL)
                            pe.wait_ge(ffn_w1_in, 16 * 3 * L)
                        if k >= K // 2 and shifts_of:
                            mm = shift_product(*shifts_of.pop(0))
                            if not shifts_of:
                                mm.then_inc(lnb_full, 1)
                    base = 3 + 3 * K
                    pe.wait_ge(v_prep, base)
                    pe.transpose(rk[0:K, 0:K], aug[:, K:2 * K], ident[0:K, 0:K]).then_inc(pe_prep, 1)
                    pe.wait_ge(v_prep, base + 1)
                    pe.matmul(pb[0:K, 0:K], rawT[:, :], UT[:, :], start=True, stop=True).then_inc(pe_prep, 1)
                    pe.wait_ge(v_prep, base + 3)
                    pe.matmul(rk[0:K, 0:1], prod[:, :], ones[0:K, 0:1], start=True, stop=True).then_inc(pe_prep, 1)
                    pe.wait_ge(small_in, 16 * N_SMALL)
                    for c in range(DC):
                        mm = pe.matmul(pb[0:K, 0:E], outbT[:, c, :], rw[:, c, :], start=(c == 0), stop=(c == DC - 1))
                    mm.then_inc(pe_prep, 1)

                    def rank(b):
                        out_ = rk[:, 0:G * E].rearrange("p (g e) -> p g e", g=G)
                        mine = hits[:, bass.ds(b, 1), :, :].rearrange("p o g e -> p (o g) e")
                        pe.wait_ge(hits_ready, b + 1)
                        pe.matmul(out_, earlier[:, :], mine, start=True, stop=False)
                        pe.matmul(out_, ones_bf[:, :], hits_before[:, :].unsqueeze(1).to_broadcast([P, G, E]),
                                  start=False, stop=False)
                        for d in range(1, G):
                            mm = pe.matmul(out_[:, d:G, :], ones_bf[:, :],
                                           hits[:, bass.ds(b, 1), 0:G - d, :].rearrange("p o g e -> p (o g) e"),
                                           start=False, stop=(d == G - 1))
                        mm.then_inc(rank_full, 1)

                    def sequence(i, par, last):
                        b = i * 2 + par
                        pe.wait_ge(x_copied, b * DC + DC)
                        for c in range(DC):
                            mm = pe.matmul(pb[0:K, :], basisT[:, c, :], xT[:, c, :], start=(c == 0), stop=(c == DC - 1))
                        mm.then_inc(proj_full, 1)
                        if not last:
                            turn_x(1 - par, i + par)
                        pe.wait_ge(projT_done, b + 1)
                        pe.matmul(pb[:, :], mtr[:, :], projT[:, :], start=True, stop=True).then_inc(hid_full, 1)
                        rank(b)
                        pe.wait_ge(hidT_done, b + 1)
                        pe.wait_ge(xo_copied, b + 1)
                        for w in range(NW):
                            mm = pe.matmul(xb[:, w, 0:D + E], hidT[:, w * P:(w + 1) * P], outb[:, :],
                                           start=True, stop=True)
                        mm.then_inc(xo_full, 1)
                    pe.wait_ge(v_prep, base + 11)
                    with pe.Fori(0, B // 2 - 1) as i:
                        for par in range(2):
                            sequence(i, par, False)
                    sequence(B // 2 - 1, 0, False)
                    sequence(B // 2 - 1, 1, True)
                    rank(B)
                    pe.wait_ge(slot_ready, B + 1)
                    pe.matmul(pb[:, 0:E], ones_bf[:, :], hits_before[:, :], start=True, stop=True
                              ).then_inc(totals, 1)

                @block.vector
                def _(v):
                    n = [0]

                    def step(ins):
                        n[0] += 1
                        ins.then_inc(v_prep, 1)
                        v.wait_ge(v_prep, n[0])
                    v.wait_ge(made, N_MADE)
                    v.wait_ge(pe_prep, 3)
                    v.tensor_copy(rawT[:, :], pb[0:K, 0:K])
                    v.tensor_copy(basisT[:, :, :], tb[1][:, 0:DC * K].rearrange("p (c k) -> p c k", c=DC))
                    v.tensor_copy(outbT[:, :, :], tb[0][:, 0:DC * K].rearrange("p (c k) -> p c k", c=DC))
                    v.tensor_copy(aug[:, K:2 * K], ident[0:K, 0:K])
                    step(v.tensor_scalar(prod[:, :], ident[0:K, 0:K], 1e-4, None, ALU.mult))
                    step(v.tensor_tensor(aug[:, 0:K], rk[0:K, 0:K], prod[:, :], ALU.add))
                    v.memset(mtr[:, K:P], 0.0)
                    for k, (s, n_) in enumerate(((xo_copied, 1), (passed, 1))):
                        v.memset(pace[:, k:k + 1], 0.0).then_inc(s, n_)
                    v.memset(pace[:, 4:10], 0.0)
                    v.memset(hits_before[:, :], 0.0)
                    v.memset(b1[:, :, :, :], 0.0)
                    v.memset(hits[:, 0, :, :], 0.0).then_inc(hits_ready, 1)
                    step(v.memset(small[:, :], 0.0))
                    for k in range(K):
                        step(v.tensor_scalar(small[:, 1:2], aug[:, k:k + 1], below[:, k:k + 1], None, ALU.mult))
                        live = slice(k, K + k + 1)
                        v.wait_ge(pe_prep, 3 + k + 1)
                        v.reciprocal(small[:, 0:1], rk[0:K, k:k + 1])
                        step(v.tensor_scalar(row[:, live], rk[0:K, live], small[:, 1:2], None, ALU.mult))
                        step(v.scalar_tensor_tensor(aug[:, live], row[:, live], small[:, 0:1], aug[:, live],
                                                    ALU.mult, ALU.add))
                    v.wait_ge(lnb_full, 1)
                    v.wait_ge(small_b, 16 * 2 * 3 * L)
                    pmv = lnb_b[:, 0:2 * L * NJ].rearrange("p (l s j) -> p l s j", l=L, s=2)
                    for j, n_ in ((slice(0, FULL), P),) + tuple((slice(j, j + 1), HJ[j]) for j in range(FULL, NJ)):
                        v.tensor_tensor(b1[0:n_, :, :, j], pmv[0:n_, :, :, j], b1raw[0:n_, :, :, j], ALU.add)
                    v.wait_ge(pe_prep, 3 + K + 1)
                    step(v.tensor_copy(UT[:, :], rk[0:K, 0:K]))
                    v.wait_ge(pe_prep, 3 + K + 2)
                    step(v.tensor_copy(mtr[:, 0:K], pb[0:K, 0:K]))
                    step(v.tensor_tensor(prod[:, :], mtr[:, 0:K], raw[:, :], ALU.mult))
                    step(v.tensor_tensor(row[:, 0:K], aug[:, 0:K], ident[0:K, 0:K], ALU.mult))
                    step(v.tensor_reduce(small[:, 2:3], row[:, 0:K], AX.X, ALU.add))
                    v.wait_ge(a_prep, 4)
                    step(v.tensor_scalar(small[:, 5:6], small[:, 4:5], small[:, 4:5], small[:, 2:3],
                                         ALU.mult, ALU.mult))
                    step(v.tensor_scalar(small[:, 6:7], small[:, 5:6], -0.5, 1.5, ALU.mult, ALU.add))
                    v.wait_ge(pe_prep, 3 + K + 3)
                    step(v.tensor_scalar(small[:, 7:8], rk[0:K, 0:1], 0.0, 2.0, ALU.is_ge, ALU.mult))
                    step(v.tensor_scalar(small[:, 8:9], small[:, 7:8], -1.0, small[:, 6:7], ALU.add, ALU.mult))
                    step(v.tensor_scalar(srow[:, :], small[:, 8:9], small[:, 4:5], None, ALU.mult))
                    v.wait_ge(pe_prep, 3 + K + 4)
                    step(v.tensor_copy(outb[:, D:D + E], pb[0:K, 0:E]))
                    v.tensor_copy(iota8[:, 0:E], iota_i[:, 0:E])
                    for dst, src in ((region, region_i), (limit, lim_i),
                                     (offset, off_i)):
                        v.tensor_copy(dst[:, :], src[:, :])
                    v.memset(iota8[:, E:E + 1], 0.0)
                    CH = 9
                    m = [0]

                    def link(b, ins):
                        m[0] += 1
                        ins.then_inc(chain, 1)
                        v.wait_ge(chain, b * CH + m[0])

                    def place(b, par):
                        v.wait_ge(rank_full, b + 1)
                        mine = hits[:, bass.ds(b, 1), :, :].rearrange("p o g e -> p (o g) e")
                        link(b, v.tensor_tensor(cand[:, :, :], rk[:, 0:G * E].rearrange("p (g e) -> p g e", g=G),
                                                region[:, 0:E].unsqueeze(1).to_broadcast([P, G, E]), ALU.add))
                        v.tensor_tensor(cand[:, :, :], cand[:, :, :], mine, ALU.mult)
                        link(b, v.tensor_reduce(hit_sum[:, :], mine.rearrange("p g e -> p e g"), AX.X, ALU.add))
                        link(b, v.tensor_reduce(slot_now[:, :], cand[:, :, :], AX.X, ALU.add))
                        v.tensor_tensor(hits_before[:, :], hits_before[:, :], hit_sum[:, :], ALU.add)
                        v.tensor_copy(slot[:, bass.ds(b, 1), :].rearrange("p o g -> p (o g)"), slot_now[:, :])
                        v.tensor_copy(idx[1 - par][:, :], slot_now[:, :]).then_inc(slot_ready, 1)

                    with v.Fori(0, B // 2) as i:
                        for par in range(2):
                            b = i * 2 + par
                            m[0] = 0
                            v.wait_ge(proj_full, b + 1)
                            v.tensor_scalar(projT[:, :], pb[0:K, :], c256[0:K, bass.ds(b, 1)], None, ALU.mult
                                            ).then_inc(projT_done, 1)
                            v.wait_ge(hid_full, b + 1)
                            v.tensor_scalar(hidT[:, :], pb[0:K, :], c64[:, bass.ds(b, 1)], srow[:, 0:1], ALU.mult,
                                            ALU.mult).then_inc(hidT_done, 1)
                            place(b, par)
                            v.wait_ge(xo_full, b + 1)
                            v.tensor_copy(lg[:, :, :], xb[:, :, D:D + E]).then_inc(lg_taken, 1)
                            v.wait_ge(lg_taken, b + 1)
                            v.memset(pace[:, 9:10], 0.0)
                            for w in range(NW):
                                last = v.max(m8[:, w, :], lg[:, w, :])
                            link(b, last)
                            v.tensor_tensor(gap[:, :], m8[:, :, 1], m8[:, :, 0], ALU.subtract).then_inc(gap_done, 1)
                            for w in range(NW):
                                last = v.max_index(i8[:, w, :], m8[:, w, :], lg[:, w, :])
                            link(b, last)
                            link(b, v.tensor_copy(i8f[:, :, :], i8[:, :, 0:2]))
                            for k in range(2):
                                last = v.tensor_tensor(
                                    hits[:, bass.ds(b + 1, 1), k * NW:(k + 1) * NW, :].rearrange("p o g e -> p (o g) e"),
                                    iota8[:, 0:E].unsqueeze(1).to_broadcast([P, NW, E]),
                                    i8f[:, :, k:k + 1].to_broadcast([P, NW, E]), ALU.is_equal)
                            last.then_inc(hits_ready, 1)
                            v.wait_ge(exp_done, b + 1)
                            link(b, v.tensor_scalar(den[:, :], eg[:, :], 1.0, 2.0, ALU.add, ALU.mult))
                            link(b, v.reciprocal(den[:, :], den[:, :]))
                            v.wait_ge(scattered[par], i * 16 * G + 16 * SPARE // 2)
                            v.tensor_copy(xo[par][:, 0, :, D], den[:, :])
                            link(b, v.tensor_tensor(xo[par][:, 1, :, D], eg[:, :], den[:, :], ALU.mult))
                            v.wait_ge(xo_copied, b + 2)
                            v.tensor_copy(xo[par][:, 1, :, 0:D], xo[par][:, 0, :, 0:D])
                            assert m[0] == CH, m[0]
                    m[0] = 0
                    place(B, 0)
                    v.wait_ge(totals, 1)
                    link(B, v.tensor_copy(count[:, :], pb[:, 0:E]))
                    v.tensor_tensor(pad_start[:, :], count[0:1, :], region[0:1, 0:E], ALU.add).then_inc(pads_ready, 1)
                    link(B, v.tensor_tensor(over[:, :, :], count[:, :].unsqueeze(2).to_broadcast([P, E, T * B // P]),
                                            limit[:, :].unsqueeze(1).to_broadcast([P, E, T * B // P]), ALU.is_gt))
                    link(B, v.tensor_reduce(tiles[:, 0:E], over[:, :, :], AX.X, ALU.add))
                    link(B, v.tensor_copy(end[:, 0:1], tiles[:, 0:1]))
                    for e in range(1, E):
                        link(B, v.tensor_tensor(end[:, e:e + 1], end[:, e - 1:e], tiles[:, e:e + 1], ALU.add))
                    v.memset(begin[:, 0:1], 0.0)
                    link(B, v.tensor_copy(begin[:, 1:E + 1], end[:, 0:E]))
                    link(B, v.tensor_scalar(end[:, :], begin[:, :], float(P), None, ALU.mult))
                    link(B, v.tensor_tensor(shift[:, :], region[:, :], end[:, :], ALU.subtract))
                    tt_ = [1, TILES, E + 1]
                    link(B, v.tensor_tensor(tile_a[:, :, :], offset[0:1, :].unsqueeze(2).to_broadcast(tt_),
                                            end[0:1, :].unsqueeze(1).to_broadcast(tt_), ALU.is_ge))
                    link(B, v.tensor_tensor(tile_b[:, :, 0:E], tile_a[:, :, 0:E], tile_a[:, :, 1:E + 1], ALU.subtract))
                    link(B, v.tensor_copy(tile_b[:, :, E:E + 1], tile_a[:, :, E:E + 1]))
                    link(B, v.tensor_tensor(tile_a[:, :, :], tile_b[:, :, :],
                                            iota8[0:1, :].unsqueeze(1).to_broadcast(tt_), ALU.mult))
                    link(B, v.tensor_reduce(tile_f[:, :], tile_a[:, :, :], AX.X, ALU.add))
                    link(B, v.tensor_copy(tile_expert[:, :], tile_f[:, :]))
                    link(B, v.tensor_tensor(tile_a[:, :, :], tile_b[:, :, :],
                                            shift[0:1, :].unsqueeze(1).to_broadcast(tt_), ALU.mult))
                    link(B, v.tensor_reduce(tile_f[:, :], tile_a[:, :, :], AX.X, ALU.add))
                    v.tensor_tensor(tile_row[:, :], tile_f[:, :], offset[0:1, :], ALU.add)
                    link(B, v.tensor_tensor(
                        cand_all[:, :, :], hits[:, 1:B + 1, :, :].rearrange("p b g e -> p (b g) e"),
                        shift[:, 0:E].unsqueeze(1).to_broadcast([P, B * G, E]), ALU.mult))
                    link(B, v.tensor_reduce(shifts[:, :], cand_all[:, :, :], AX.X, ALU.add))
                    v.tensor_tensor(y_row[:, :, :], slot[:, 1:B + 1, :],
                                    shifts[:, :].rearrange("p (b g) -> p b g", b=B), ALU.subtract)

                @block.scalar
                def _(a):
                    for l in range(L):
                        for side in range(2):
                            f = side * HID
                            a.dma_start(b1raw[:, l, side, 0:FULL],
                                        L1_ffn_b1[l, f:f + FULL * P].rearrange("(j p) -> p j", p=P),
                                        allow_slow_non_contiguous=True).then_inc(small_b, 16)
                            for j in range(FULL, NJ):
                                a.dma_start(b1raw[0:HJ[j], l, side, j:j + 1],
                                            L1_ffn_b1[l, f + AT[j]:f + AT[j] + HJ[j]].rearrange("(p o) -> p o", o=1),
                                            allow_slow_non_contiguous=True).then_inc(small_b, 16)
                    a.preload_act_table_set("natural_log_exp_and_others")
                    def copy_x(b):
                        for c in range(DC):
                            a.wait_ge(x_full, b * DC + (c + 1))
                            a.copy(xT[:, c, :], tb[c][:, :]).then_inc(x_copied, 1)

                    def sequence(i, par, last):
                        b = i * 2 + par
                        if not last:
                            copy_x(b + 1)
                        a.wait_ge(lg_taken, b + 1)
                        a.wait_ge(scattered[par], i * 16 * G + 16 * SPARE // 2)
                        a.copy(xo[par][:, 0, :, 0:D], xb[:, :, 0:D]).then_inc(xo_copied, 1)
                        a.wait_ge(gap_done, b + 1)
                        a.activation(eg[:, :], gap[:, :], ACT.Exp).then_inc(exp_done, 1)
                    a.wait_ge(p_prep, PREP_QN)
                    a.activation(ss[:, 2:4], ss[:, 0:2], ACT.Ln).then_inc(a_prep, 1)
                    a.wait_ge(a_prep, 1)
                    a.activation(ss[:, 2:4], ss[:, 2:4], ACT.Exp, scale=-0.5).then_inc(a_prep, 1)
                    copy_x(0)
                    base = 3 + 3 * K
                    a.wait_ge(v_prep, base + 5)
                    a.activation(small[:, 3:4], small[:, 2:3], ACT.Ln).then_inc(a_prep, 1)
                    a.wait_ge(a_prep, 3)
                    a.activation(small[:, 4:5], small[:, 3:4], ACT.Exp, scale=-0.5).then_inc(a_prep, 1)
                    with a.Fori(0, B // 2 - 1) as i:
                        for par in range(2):
                            sequence(i, par, False)
                    sequence(B // 2 - 1, 0, False)
                    sequence(B // 2 - 1, 1, True)

        with ExitStack() as st:
            sb, ps, sem = scope(st)
            NB = 6
            xt = [sb(f"xt{i}", [P, XW]) for i in range(NB)]
            xs = [sb(f"xs{i}", [P, DC, P]) for i in range(2)]
            tanh = [sb(f"tanh{i}", [P, F]) for i in range(2)]
            hp = [sb(f"hp{i}", [P, F]) for i in range(2)]
            hT = [sb(f"hT{i}", [P, FC, P]) for i in range(2)]
            yt = [sb(f"yt{i}", [P, D]) for i in range(NB)]
            pace = sb("pace_e", [P, NB + 1])
            xb = [ps(f"xsb{i}", [P, DC, P]) for i in range(2)]
            ub = [ps(f"ub{i}", [P, F]) for i in range(2)]
            tb = [ps(f"hTb{i}", [P, FC, P]) for i in range(2)]
            yb = [ps(f"yb{i}", [P, 512]) for i in range(2)]

            tile_in = [sem(f"tile_in{i}") for i in range(NB)]
            y_stored = [sem(f"y_stored{i}") for i in range(NB)]
            x_full = sem("x_full_e")
            xs_done = sem("xs_done")
            u_full = sem("u_full")
            tanh_done = sem("tanh_done")
            hp_ready = sem("hp_ready")
            t_full = sem("t_full")
            hT_done = sem("hT_done")
            y_full = sem("y_full")
            y_copied = sem("y_copied")

            def tiles_walk(eng, one):
                with eng.Fori(0, TILES // NB - 1) as i:
                    for k in range(NB):
                        one(i * NB + k, k, i, TILES)
                for k in range(NB):
                    one(TILES - NB + k, k, TILES // NB - 1, NB - k)

            with nc.Block() as block:
                @block.sync
                def _(sp):
                    def row_of(t):
                        return sp.value_load(tile_row[0:1, bass.ds(t, 1)], min_val=0, max_val=SLOTS - P)

                    def load(k, first_row):
                        sp.dma_start(xt[k][:, :], slots_x[bass.ds(first_row, P), :]).then_inc(tile_in[k], 16)
                    for t in range(NB):
                        load(t, row_of(t))
                    sp.dma_start(x1tok[:, :, :], XROW[0]).then_inc(loaded, 16)

                    def one(t, k, i, left):
                        sp.wait_ge(y_copied, t + 3)
                        sp.dma_start(SY[t], yt[k][:, :]).then_inc(y_stored[k], 16)
                        if left > NB:
                            load(k, row_of(t + NB))
                    tiles_walk(sp, one)
                    for s in y_stored:
                        sp.wait_ge(s, 16 * (TILES // NB + 1))

                @block.tensor
                def _(pe):
                    def turn_x(t, k, n):
                        pe.wait_ge(tile_in[k], n * 16 + 16)
                        for c in range(DC):
                            mm = pe.transpose(xb[k % 2][:, c, :], xt[k][:, c * P:(c + 1) * P], ident[:, :])
                        mm.then_inc(x_full, 1)

                    expert_of = {}

                    def up(t, k):
                        e = expert_of[k] = pe.value_load(tile_expert[0:1, bass.ds(t, 1)], min_val=0, max_val=E - 1)
                        pe.wait_ge(xs_done, t + 1)
                        for c in range(DC):
                            mm = pe.matmul(ub[k % 2][:, :], xs[k % 2][:, c, :],
                                           w1m[:, bass.ds(e, 1), c, :].rearrange("p o f -> p (o f)"),
                                           start=(c == 0), stop=(c == DC - 1))
                        mm.then_inc(u_full, 1)

                    def one(t, k, i, left):
                        if left > 2:
                            turn_x(t + 2, (k + 2) % NB, i + (k + 2) // NB)
                        pe.wait_ge(hp_ready, t + 1)
                        for j in range(FC):
                            mm = pe.transpose(tb[k % 2][:, j, :], hp[k % 2][:, j * P:(j + 1) * P], ident[:, :])
                        mm.then_inc(t_full, 1)
                        if left > 1:
                            up(t + 1, k + 1)
                        e = expert_of.pop(k, None) if k else None
                        if e is None:
                            e = pe.value_load(tile_expert[0:1, bass.ds(t, 1)], min_val=0, max_val=E - 1)
                        pe.wait_ge(hT_done, t + 1)
                        pe.wait_ge(y_copied, t + 1)
                        for j in range(FC):
                            mm = pe.matmul(yb[k % 2][:, 0:D], hT[k % 2][:, j, :],
                                           w2m[:, bass.ds(e, 1), j, :].rearrange("p o d -> p (o d)"),
                                           start=(j == 0), stop=(j == FC - 1))
                        mm.then_inc(y_full, 1)

                    pe.wait_ge(expert_w, 16 * 2 * E)
                    turn_x(0, 0, 0)
                    turn_x(1, 1, 0)
                    up(0, 0)
                    tiles_walk(pe, one)

                @block.vector
                def _(v):
                    for k in range(NB):
                        v.memset(pace[:, k:k + 1], 0.0).then_inc(y_stored[k], 16)
                    v.memset(pace[:, NB:NB + 1], 0.0).then_inc(y_copied, 2)

                    def silu(t, k):
                        v.wait_ge(tanh_done, t + 1)
                        v.scalar_tensor_tensor(hp[k % 2][:, :], tanh[k % 2][:, :], 1.0, ub[k % 2][:, :],
                                               ALU.add, ALU.mult).then_inc(hp_ready, 1)

                    def one(t, k, i, left):
                        if left > 1:
                            silu(t + 1, k + 1)
                        v.wait_ge(y_full, t + 1)
                        v.wait_ge(y_stored[k], i * 16 + 16)
                        v.tensor_scalar(yt[k][:, :], yb[k % 2][:, 0:D], xt[k][:, D:D + 1], None, ALU.mult
                                        ).then_inc(y_copied, 1)
                    silu(0, 0)
                    tiles_walk(v, one)

                @block.scalar
                def _(a):
                    a.preload_act_table_set("exp_and_others")

                    def copy_x(t, k):
                        a.wait_ge(x_full, t + 1)
                        a.copy(xs[k % 2][:, :, :], xb[k % 2][:, :, :]).then_inc(xs_done, 1)

                    def act(t, k):
                        a.wait_ge(u_full, t + 1)
                        a.activation(tanh[k % 2][:, :], ub[k % 2][:, :], ACT.Tanh, scale=0.5).then_inc(tanh_done, 1)

                    def one(t, k, i, left):
                        if left > 2:
                            copy_x(t + 2, k + 2)
                        a.wait_ge(t_full, t + 1)
                        a.copy(hT[k % 2][:, :, :], tb[k % 2][:, :, :]).then_inc(hT_done, 1)
                        if left > 1:
                            act(t + 1, k + 1)
                    copy_x(0, 0)
                    copy_x(1, 1)
                    act(0, 0)
                    tiles_walk(a, one)
        experts.close()


        with ExitStack() as st:
            sb, ps, sem = scope(st)
            xT = [sb(f"xT{s}", [P, DC, T + 1]) for s in range(2)]
            rows = sb("rows", [P, G], U32)
            no_rows = sb("no_rows", [P, G], U32)
            pace = sb("pace_l", [P, 2])
            x1out = sb("x1out", [P, NW, D])
            outt = sb("outt", [P, NW, D])
            x1T = sb("x1T", [P, DC, T])
            raw = sb("qkraw", [P, 2, 2, INNER])
            qksq = sb("qksq", [P, 2 * INNER])
            ss = sb("ssum", [P, 2 * H])
            lns = sb("lns", [P, 2 * H])
            rn = sb("rn", [P, 2 * H])
            direct = sb("direct", [P, 2, INNER])
            swapped = sb("swapped", [P, 2, INNER])
            roped = sb("roped", [P, 2, INNER])
            vv = sb("vv", [P, 4, INNER])
            qT = sb("qT", [P, IC, P])
            kT = sb("kT", [P, IC, 2, P])
            nm = sb("nm", [P, 4, 2])
            prob = sb("prob", [P, 4, 2, 2 * P])
            rs = sb("rs", [P, 2, H])
            rr = sb("rr", [P, H])
            pT = sb("pT", [P, 4, 2, 2, P])
            on = sb("on", [P, INNER])
            oT = sb("oT", [P, IC, T])
            xc = sb("xc", [P, DC, T])
            xsq = sb("xsq", [P, DC, T])
            lnv = sb("lnv", [P, T])
            rstd = sb("rstd", [P, T])
            h = sb("h", [P, DC, T])
            gb = sb("gb", [P, NJ, T])
            hid = sb("hid", [P, NJ, T])

            pj = [ps(f"pj{i}", [P, 512]) for i in range(NP)]
            sc = [ps(f"sc{i}", [P, 2, 2 * P]) for i in range(2)]
            pt = [ps(f"pt{i}", [P, 2, 2, P]) for i in range(2)]
            ob = ps("ob", [P, INNER])

            proj_full = sem("proj_full")
            proj_taken = [sem(f"proj_taken{i}") for i in range(NP)]
            squared = sem("squared")
            edge = sem("edge")
            summed = sem("summed")
            floored = sem("floored")
            logged = sem("logged")
            norm_ready = sem("norm_ready")
            parts_ready = sem("parts_ready")
            added = sem("added")
            rope_done = sem("rope_done")
            s_full = sem("s_full")
            max_done = sem("max_done")
            exp_done = sem("exp_done")
            pt_full = sem("pt_full")
            pt_taken = [sem(f"pt_taken{i}") for i in range(2)]
            pv_done = sem("pv_done")
            inverted = sem("inverted")
            o_ready = sem("o_ready")
            xsq_ready = sem("xsq_ready")
            rstd_ready = sem("rstd_ready")
            h_ready = sem("h_ready")
            gelu_done = sem("gelu_done")
            reloaded = sem("reloaded")
            picked = [sem(f"picked{k}") for k in range(TOP)]
            rows_ready = sem("rows_ready")
            kept = sem("kept")
            passed = sem("passed_l")
            saved = sem("saved")

            def at(count, i, per_body, mul=1, add=0):
                return i * (per_body * mul) + (count * mul + add)

            def wait(eng, s, value):
                if not (isinstance(value, int) and value <= 0):
                    eng.wait_ge(s, value)

            def wait_taken(eng, u, i):
                eng.wait_ge(proj_taken[u % NP], at(u // NP, i, USE // NP, 1, 1))

            def wait_full(eng, u, i):
                eng.wait_ge(proj_full, at(u, i, USE, 1, 1))
                return pj[u % NP]

            def xs(s, c, t0=0, n=T):
                return xT[s][:, c, 1 - c + t0:1 - c + t0 + n]

            def walk(eng, one):
                for st in first:
                    one(st, 0)
                with eng.Fori(0, ITER - 1) as i:
                    for st in body:
                        one(st, i)
                for st in last:
                    one(st, ITER - 1)

            def move_p(eng, copy, st, i):
                g = st["grp"]
                n = 2 if st["w"] else 1
                eng.wait_ge(pt_full, at(g, i, GRP, 1, 1))
                wait(eng, pv_done, at(g, i, GRP, 1, -3))
                copy(pT[:, g % 4, :, 0:n, :], pt[g % 2][:, :, 0:n, :]).then_inc(pt_taken[g % 2], 1)

            with nc.Block() as block:
                @block.sync
                def _(sp):
                    def fetch(n):
                        sp.dma_start(x1tok[:, :, :], XROW[n]).then_inc(loaded, 16)

                    def fetch_again(n):
                        sp.dma_start(x1out[:, :, :], x1[n]).then_inc(reloaded, 16)

                    def one(st, i, last_out=False, fetch_first=False):
                        if st["kind"] == "pick" and st["k"] == TOP - 1:
                            n = i * 2 + st["pick"]
                            sp.wait_ge(picked[TOP - 1], at(st["pick"], i, LOADS, 16 * NW, 16 * NW))
                            sp.dma_start(x1[n], x1tok[:, :, :]).then_inc(kept, 16)
                            if fetch_first:
                                sp.wait_ge(kept, 16)
                                fetch_again(0)
                        elif st["kind"] == "load" and st["load"] % 2 == 0:
                            wait_full(sp, st["use"] + 1, i)
                            fetch(i * 2 + (st["load"] + 1))
                        elif st["kind"] == "out":
                            wait_taken(sp, st["use"] + NW - 1, i)
                            sp.dma_start(out[i * 2 + st["outs"]].rearrange("(w p) d -> p w d", p=P), outt[:, :, :]
                                         ).then_inc(saved, 16)
                            if not last_out:
                                fetch_again(i * 2 + (st["outs"] + 1))
                    for st in first:
                        one(st, 0, fetch_first=st["kind"] == "pick" and st["pick"] == 0)
                    with sp.Fori(0, ITER - 1) as i:
                        wait_full(sp, body[0]["use"] - 1, i)
                        fetch(i * 2 + 2)
                        for st in body:
                            one(st, i)
                    for st in last:
                        one(st, ITER - 1, last_out=st["outs"] == OUTS - 1)
                    sp.wait_ge(saved, 16 * (B + 1))

                @block.tensor
                def _(pe):
                    pe.wait_ge(edge, 1)

                    def bank(u, i):
                        wait(pe, proj_taken[u % NP], at(u // NP, i, USE // NP))
                        return pj[u % NP]

                    def one(st, i):
                        kind, s, u = st["kind"], st["s"], st["use"]
                        l, w = st.get("l"), st.get("w")
                        if kind == "load":
                            pe.wait_ge(kept, at(st["load"], i, LOADS, 16, 16)) if st["load"] else pe.wait_ge(
                                picked[TOP - 1], 16 * NW)
                            for c in range(DC):
                                o = bank(u + c, i)
                                for k in range(NW):
                                    mm = pe.transpose(o[:, k * P:(k + 1) * P], x1tok[:, k, c * P:(c + 1) * P],
                                                      ident[:, :])
                                mm.then_inc(proj_full, 1)
                        elif kind == "rotate":
                            wait_taken(pe, st["load_use"] - 1, i)
                            wait_taken(pe, st["load_use"], i)
                            for co in range(DC):
                                o = bank(u + co, i)
                                for c in range(DC):
                                    mm = pe.matmul(o[:, :], rot[:, c, co * P:(co + 1) * P], x1T[:, c, :],
                                                   start=(c == 0), stop=(c == DC - 1))
                                mm.then_inc(proj_full, 1)
                        elif kind == "qkv":
                            if w == 0:
                                wait_taken(pe, st["x_use"] - 1, i)
                                wait_taken(pe, st["x_use"], i)
                            for k in range(3):
                                o = bank(u + k, i)
                                for c in range(DC):
                                    mm = pe.matmul(o[:, :], xs(s, c, w * P, P), wqkv[:, l, c, k * INNER:(k + 1) * INNER],
                                                   start=(c == 0), stop=(c == DC - 1))
                                mm.then_inc(proj_full, 1)
                        elif kind == "turn":
                            for k in range(2):
                                o = bank(u + k, i)
                                pe.wait_ge(rope_done, at(st["win"], i, WIN, 2, k + 1))
                                for c in range(IC):
                                    mm = pe.transpose(o[:, c * P:(c + 1) * P], roped[:, k, c * P:(c + 1) * P],
                                                      ident[:, :])
                                mm.then_inc(proj_full, 1)
                        elif kind == "score":
                            g = st["grp"]
                            wait(pe, exp_done, at(g, i, GRP, 1, -1))
                            if st["g"] == 0:
                                wait_taken(pe, st["turn_use"] - 1, i)
                                wait_taken(pe, st["turn_use"], i)
                            o = sc[g % 2]
                            n = 2 * P if w else P
                            pe.matmul(o[:, :, 0:n], ident_bf[:, :], mask[:, w % 2, :, 0:n], start=True, stop=False,
                                      skip_group_check=True)
                            for hh in range(2):
                                head = head_of(st["g"], hh)
                                r = slice(DH * (head % 2), DH * (head % 2) + DH)
                                mm = pe.matmul(o[:, hh, 0:n], qT[r, head // 2, :],
                                               kT[r, head // 2, :, :].rearrange("p a b -> p (a b)")[:, 0:n],
                                               start=False, stop=True, skip_group_check=True)
                            mm.then_inc(s_full, 1)
                        elif kind == "turn_p":
                            g = st["grp"]
                            pe.wait_ge(exp_done, at(g, i, GRP, 1, 1))
                            wait(pe, pt_taken[g % 2], at(g // 2, i, GRP // 2))
                            for hh in range(2):
                                for k in range(2 if w else 1):
                                    mm = pe.transpose(pt[g % 2][:, hh, k, :], prob[:, g % 4, hh, k * P:(k + 1) * P],
                                                      ident[:, :])
                            mm.then_inc(pt_full, 1)
                        elif kind == "pv":
                            g, win = st["grp"], st["win"]
                            pe.wait_ge(pt_taken[g % 2], at(g // 2, i, GRP // 2, 1, 1))
                            if st["g"] == 0:
                                wait(pe, o_ready, at(win, i, WIN))
                            for hh in range(2):
                                head = head_of(st["g"], hh)
                                slots = [(w % 2, win % 4)] + ([(1 - w % 2, (win - 1) % 4)] if w else [])
                                for k, (slot, v_at) in enumerate(slots):
                                    mm = pe.matmul(ob[:, head * DH:(head + 1) * DH], pT[:, g % 4, hh, slot, :],
                                                   vv[:, v_at, head * DH:(head + 1) * DH],
                                                   start=(k == 0), stop=(k == len(slots) - 1))
                            mm.then_inc(pv_done, 1)
                        elif kind == "turn_o":
                            pe.wait_ge(o_ready, at(st["win"], i, WIN, 1, 1))
                            o = bank(u, i)
                            for c in range(IC):
                                mm = pe.transpose(o[:, c * P:(c + 1) * P], on[:, c * P:(c + 1) * P], ident[:, :])
                            mm.then_inc(proj_full, 1)
                        elif kind == "wo":
                            wait_taken(pe, st["turn_o_use"], i)
                            o = bank(u, i)
                            for k in range(IC):
                                mm = pe.matmul(o[:, :], wo[:, l, k, st["c"] * P:(st["c"] + 1) * P], oT[:, k, :],
                                               start=(k == 0), stop=(k == IC - 1))
                            mm.then_inc(proj_full, 1)
                        elif kind == "mean":
                            wait_taken(pe, st["wo_use"], i)
                            o = bank(u, i)
                            for c in range(DC):
                                mm = pe.matmul(o[:, :], mean_w[:, :], xs(s, c), start=(c == 0), stop=(c == DC - 1))
                            mm.then_inc(proj_full, 1)
                        elif kind == "var":
                            pe.wait_ge(xsq_ready, at(st["ffn"], i, FFN, 1, 1))
                            o = bank(u, i)
                            for c in range(DC):
                                mm = pe.matmul(o[:, :], mean_w[:, :], xsq[:, c, :], start=(c == 0), stop=(c == DC - 1))
                            mm.then_inc(proj_full, 1)
                        elif kind in ("gate", "value"):
                            j = st["j"]
                            pe.wait_ge(h_ready, at(st["ffn"], i, FFN, DC, DC))
                            o = bank(u, i)
                            for c in range(DC):
                                if j == NJ - 1:
                                    cols = w1[:, l, c, AT[j]:AT[j] + P]
                                else:
                                    f = (GATE_AT if kind == "gate" else AT)[j]
                                    cols = w1[:, l, c, f:f + HJ[j]]
                                mm = pe.matmul(o[0:P if j == NJ - 1 else HJ[j], :], cols, h[:, c, :], start=(c == 0), stop=(c == DC - 1))
                            mm.then_inc(proj_full, 1)
                        elif kind == "down":
                            wait_taken(pe, st["value_use"], i)
                            o = bank(u, i)
                            for j in range(NJ):
                                mm = pe.matmul(o[:, :], w2[0:HJ[j], l, j, st["c"] * P:(st["c"] + 1) * P],
                                               hid[0:HJ[j], j, :], start=(j == 0), stop=(j == NJ - 1))
                            mm.then_inc(proj_full, 1)
                        elif kind == "out":
                            wait_taken(pe, st["x_use"] - 1, i)
                            wait_taken(pe, st["x_use"], i)
                            for w_ in range(NW):
                                o = bank(u + w_, i)
                                for c in range(DC):
                                    mm = pe.transpose(o[:, c * P:(c + 1) * P], xT[s][:, c, 1 + w_ * P:1 + (w_ + 1) * P],
                                                      ident[:, :])
                                mm.then_inc(proj_full, 1)
                    walk(pe, one)

                @block.scalar
                def _(a):
                    a.preload_act_table_set("natural_log_exp_and_others")

                    def one(st, i):
                        kind, s, u = st["kind"], st["s"], st["use"]
                        l, w = st.get("l"), st.get("w")
                        if kind in ("load", "rotate"):
                            for c in range(DC):
                                o = wait_full(a, u + c, i)
                                dst = x1T[:, c, :] if kind == "load" else xT[s][:, c, 1:T + 1]
                                a.copy(dst, o[:, :]).then_inc(proj_taken[(u + c) % NP], 1)
                        elif kind == "qkv":
                            wait(a, parts_ready, at(st["win"], i, WIN, 2, -2))
                            for k in range(3):
                                if k == 2:
                                    wait(a, pv_done, at(st["win"], i, WIN, 4, -8))
                                o = wait_full(a, u + k, i)
                                dst = raw[:, st["win"] % 2, k, :] if k < 2 else vv[:, st["win"] % 4, :]
                                a.copy(dst, o[:, :]).then_inc(proj_taken[(u + k) % NP], 1)
                        elif kind == "norm":
                            win = st["win"]
                            a.wait_ge(floored, at(win, i, WIN, 1, 1))
                            a.activation(lns[:, :], ss[:, :], ACT.Ln, scale=LN_SHIFT).then_inc(logged, 1)
                            a.wait_ge(logged, at(win, i, WIN, 1, 1))
                            a.activation(rn[:, :], lns[:, :], ACT.Exp, scale=-0.5, bias=consts[:, 1:2]
                                         ).then_inc(norm_ready, 1)
                        elif kind == "turn":
                            wait(a, s_full, at(st["win"], i, WIN, 4))
                            for k in range(2):
                                o = wait_full(a, u + k, i)
                                dst = kT[:, :, st["win"] % 2, :] if k else qT[:, :, :]
                                a.copy(dst, o[:, :].rearrange("p (c t) -> p c t", c=IC)
                                       ).then_inc(proj_taken[(u + k) % NP], 1)
                        elif kind == "score":
                            g = st["grp"]
                            n = 2 * P if w else P
                            a.wait_ge(max_done, at(g, i, GRP, 1, 1))
                            wait(a, pt_full, at(g, i, GRP, 1, -3))
                            for hh in range(2):
                                head = head_of(st["g"], hh)
                                ins = a.activation(prob[:, g % 4, hh, 0:n], sc[g % 2][:, hh, 0:n], ACT.Exp,
                                                   bias=nm[:, g % 4, hh:hh + 1],
                                                   accum_out=rs[:, st["win"] % 2, head:head + 1])
                            ins.then_inc(exp_done, 1)
                        elif kind == "turn_p":
                            if st["grp"] % 2:
                                move_p(a, a.copy, st, i)
                        elif kind == "turn_o":
                            o = wait_full(a, u, i)
                            a.copy(oT[:, :, w * P:(w + 1) * P], o[:, :].rearrange("p (c t) -> p c t", c=IC)
                                   ).then_inc(proj_taken[u % NP], 1)
                        elif kind == "mean":
                            wait_taken(a, u, i)
                            a.activation(xsq[:, :, :], xc[:, :, :], ACT.Square).then_inc(xsq_ready, 1)
                        elif kind == "var":
                            o = wait_full(a, u, i)
                            a.activation(lnv[:, :], o[:, :], ACT.Ln, bias=consts[:, 0:1]).then_inc(proj_taken[u % NP], 1)
                            wait_taken(a, u, i)
                            a.activation(rstd[:, :], lnv[:, :], ACT.Exp, scale=-0.5).then_inc(rstd_ready, 1)
                        elif kind == "gate":
                            j = st["j"]
                            o = wait_full(a, u, i)
                            if j == NJ - 1:
                                a.activation(hid[0:HJ[j], j, :], o[0:HJ[j], :], ACT.Identity,
                                             bias=b1[0:HJ[j], l, 0, j:j + 1])
                                a.copy(gb[0:HJ[j], j, :], o[HJ[j]:P, :]).then_inc(proj_taken[u % NP], 1)
                            else:
                                a.activation(gb[0:HJ[j], j, :], o[0:HJ[j], :], ACT.Identity,
                                             bias=b1[0:HJ[j], l, 1, j:j + 1]).then_inc(proj_taken[u % NP], 1)
                        elif kind == "gelu":
                            wait_taken(a, st["gate_use"], i)
                            a.activation(gb[:, 0:NJ - 1, :], gb[:, 0:NJ - 1, :], ACT.Gelu)
                            a.activation(gb[0:HJ[-1], NJ - 1, :], gb[0:HJ[-1], NJ - 1, :], ACT.Gelu,
                                         bias=b1[0:HJ[-1], l, 1, NJ - 1:NJ]).then_inc(gelu_done, 1)
                            a.preload_act_table_set("natural_log_exp_and_others")
                    walk(a, one)

                @block.gpsimd
                def _(pool):
                    pool.memset(gb[:, FULL, :], 0.0)
                    for s in range(2):
                        ins = pool.memset(xT[s][:, :, 0:1], 0.0)
                    ins.then_inc(edge, 1)
                    pool.memset(no_rows[:, :], 0)
                    pool.memset(pace[:, :], 0.0).then_inc(passed, 1)
                    pool.wait_ge(passed, 1)

                    def one(st, i):
                        kind = st["kind"]
                        if kind == "pick":
                            n, k = st["pick"], st["k"]
                            if k == 0:
                                pool.wait_ge(loaded, at(n, i, LOADS, 16, 16))
                                pool.tensor_tensor(rows[:, :], y_row[:, bass.ds(i * LOADS + n, 1), :].rearrange(
                                    "p o g -> p (o g)"), no_rows[:, :], ALU.add).then_inc(rows_ready, 1)
                                pool.wait_ge(rows_ready, at(n, i, LOADS, 1, 1))
                            else:
                                pool.wait_ge(picked[k - 1], at(n, i, LOADS, 16 * NW, 16 * NW))
                            pool.wait_ge(passed, at(n, i, LOADS, 2, k + 1))
                            pool.tensor_tensor(pace[:, 0:1], pace[:, 1:2], pace[:, 1:2], ALU.add).then_inc(passed, 1)
                            for w in range(NW):
                                g = k * NW + w
                                pool.indirect_dma_start(
                                    out=x1tok[:, w, :], out_offset=None, in_=slots_y,
                                    in_offset=bass.IndirectOffsetOnAxis(ap=rows[:, g:g + 1], axis=0),
                                    compute_op=ALU.add).then_inc(picked[k], 16)
                        if kind == "qkv":
                            for k in range(2):
                                wait_taken(pool, st["use"] + k, i)
                                if k == 0:
                                    wait(pool, summed, at(st["win"], i, WIN))
                                src = raw[:, st["win"] % 2, k, :]
                                pool.tensor_tensor(qksq[:, k * INNER:(k + 1) * INNER], src, src, ALU.mult
                                                   ).then_inc(squared, 1)
                        elif kind == "rope":
                            for k in range(2):
                                n = 2 * st["win"] + k
                                pool.wait_ge(parts_ready, at(n, i, 2 * WIN, 1, 1))
                                pool.tensor_tensor(direct[:, k, :], direct[:, k, :], swapped[:, k, :], ALU.add
                                                   ).then_inc(added, 1)
                        elif kind == "norm":
                            for k in range(2):
                                n = 2 * st["win"] + k
                                pool.wait_ge(added, at(n, i, 2 * WIN, 1, 1))
                                if k == 0:
                                    pool.wait_ge(norm_ready, at(st["win"], i, WIN, 1, 1))
                                pool.tensor_tensor(
                                    roped[:, k, :].rearrange("p (h d) -> p h d", h=H),
                                    direct[:, k, :].rearrange("p (h d) -> p h d", h=H),
                                    rn[:, k * H:(k + 1) * H].unsqueeze(2).to_broadcast([P, H, DH]), ALU.mult
                                ).then_inc(rope_done, 1)
                    walk(pool, one)

                @block.vector
                def _(v):
                    v.memset(outt[:, :, :], 0.0).then_inc(saved, 16)

                    def one(st, i):
                        kind, s, u = st["kind"], st["s"], st["use"]
                        l, w = st.get("l"), st.get("w")
                        if kind == "rope":
                            win = st["win"]
                            wait(v, rope_done, at(win, i, WIN, 2))
                            for k in range(2):
                                wait_taken(v, st["qkv_use"] - 2 + k, i)
                                src = raw[:, win % 2, k, :].rearrange("p (h d) -> p h d", h=H)
                                t = tabs[:, l, 2 * k, w, :].unsqueeze(1).to_broadcast([P, H, DH])
                                v.tensor_tensor(direct[:, k, :].rearrange("p (h d) -> p h d", h=H), src, t, ALU.mult)
                                sw = swapped[:, k, :].rearrange("p (h d) -> p h d", h=H)
                                for half in range(2):
                                    d0, s0 = half * DH // 2, (1 - half) * DH // 2
                                    t = tabs[:, l, 2 * k + 1, w, d0:d0 + DH // 2].unsqueeze(1).to_broadcast([P, H, DH // 2])
                                    ins = v.tensor_tensor(sw[:, :, d0:d0 + DH // 2], src[:, :, s0:s0 + DH // 2], t,
                                                          ALU.mult)
                                ins.then_inc(parts_ready, 1)
                        elif kind == "norm":
                            win = st["win"]
                            v.wait_ge(squared, at(win, i, WIN, 2, 2))
                            v.tensor_reduce(ss[:, :], qksq[:, :].rearrange("p (h d) -> p h d", h=2 * H), AX.X, ALU.add
                                            ).then_inc(summed, 1)
                            v.wait_ge(summed, at(win, i, WIN, 1, 1))
                            v.tensor_scalar(ss[:, :], ss[:, :], NORM_FLOOR, None, ALU.max).then_inc(floored, 1)
                        elif kind == "score":
                            g = st["grp"]
                            n = 2 * P if w else P
                            v.wait_ge(s_full, at(g, i, GRP, 1, 1))
                            v.tensor_reduce(nm[:, g % 4, :], sc[g % 2][:, :, 0:n], AX.X, ALU.max, negate=True
                                            ).then_inc(max_done, 1)
                        elif kind == "turn_p":
                            if st["grp"] % 2 == 0:
                                move_p(v, v.tensor_copy, st, i)
                        elif kind == "pv" and st["g"] == 3:
                            win = st["win"]
                            v.wait_ge(pv_done, at(win, i, WIN, 4, 4))
                            v.reciprocal(rr[:, :], rs[:, win % 2, :]).then_inc(inverted, 1)
                            v.wait_ge(inverted, at(win, i, WIN, 1, 1))
                            v.tensor_tensor(on[:, :].rearrange("p (h d) -> p h d", h=H),
                                            ob[:, :].rearrange("p (h d) -> p h d", h=H),
                                            rr[:, :].unsqueeze(2).to_broadcast([P, H, DH]), ALU.mult
                                            ).then_inc(o_ready, 1)
                        elif kind == "wo":
                            o = wait_full(v, u, i)
                            x_ = xT[s][:, st["c"], 1:T + 1]
                            v.tensor_tensor(x_, o[:, :], x_, ALU.add).then_inc(proj_taken[u % NP], 1)
                        elif kind == "mean":
                            o = wait_full(v, u, i)
                            for c in range(DC):
                                ins = v.tensor_tensor(xc[:, c, :], xs(s, c), o[:, :], ALU.subtract)
                            ins.then_inc(proj_taken[u % NP], 1)
                        elif kind == "hnorm":
                            v.wait_ge(rstd_ready, at(st["ffn"], i, FFN, 1, 1))
                            for c in range(DC):
                                v.scalar_tensor_tensor(h[:, c, :], xc[:, c, :], lng[:, l, c:c + 1], rstd[:, :],
                                                       ALU.mult, ALU.mult).then_inc(h_ready, 1)
                        elif kind == "value":
                            j = st["j"]
                            if j == 0:
                                v.wait_ge(gelu_done, at(st["ffn"], i, FFN, 1, 1))
                                v.tensor_tensor(hid[0:HJ[-1], NJ - 1, :], hid[0:HJ[-1], NJ - 1, :],
                                                gb[0:HJ[-1], NJ - 1, :], ALU.mult)
                            o = wait_full(v, u, i)
                            v.scalar_tensor_tensor(hid[0:HJ[j], j, :], o[0:HJ[j], :], b1[0:HJ[j], l, 0, j:j + 1],
                                                   gb[0:HJ[j], j, :], ALU.add, ALU.mult).then_inc(proj_taken[u % NP], 1)
                        elif kind == "down":
                            o = wait_full(v, u, i)
                            x_ = xT[s][:, st["c"], 1:T + 1]
                            v.scalar_tensor_tensor(x_, o[:, :], b2[:, l, st["c"]:st["c"] + 1], x_, ALU.add, ALU.add
                                                   ).then_inc(proj_taken[u % NP], 1)
                        elif kind == "out":
                            v.wait_ge(saved, at(st["outs"], i, OUTS, 16, 16))
                            v.wait_ge(reloaded, at(st["outs"], i, OUTS, 16, 16))
                            for w_ in range(NW):
                                o = wait_full(v, u + w_, i)
                                v.tensor_tensor(outt[:, w_, :], o[:, 0:D], x1out[:, w_, :], ALU.add
                                                ).then_inc(proj_taken[(u + w_) % NP], 1)
                    walk(v, one)


def rotary_tables():
    f = np.float32
    half = np.arange(0, DH, 2, dtype=f)
    inv_freq = (f(1.0) / np.power(f(10000.0), half / f(DH))).astype(f)
    t = np.arange(T, dtype=f)
    freqs = t[:, None] * inv_freq[None, :]
    freqs = np.concatenate([freqs, freqs], axis=-1)
    base = ((half + f(0.4 * DH)) / f(1.4 * DH)).astype(f)
    power = ((t - f(T // 2)) / f(64.0)).astype(f)
    scale = np.power(base[None, :], power[:, None]).astype(f)
    scale = np.concatenate([scale, scale], axis=-1)
    cos, sin = np.cos(freqs), np.sin(freqs)
    sign = np.where(np.arange(DH) < DH // 2, f(-1.0), f(1.0))[None, :]
    return np.ascontiguousarray(np.stack([f(8.0) * cos * scale, f(8.0) * sin * scale * sign,
                                          cos / scale, sin / scale * sign]).astype(f))


_INS = ["x", "cond_256", "cond_64", "L0_cond_input_basis", "L0_cond_mode_to_rank", "L0_cond_output_basis",
        "L0_ffn_router_w", "L0_ffn_w1", "L0_ffn_w2", "L1_cond_q_right", "L1_cond_spectral_gate",
        "L1_ffn_wqkv", "L1_ffn_q_scale", "L1_ffn_k_scale", "L1_ffn_wo", "L1_ffn_ln_g", "L1_ffn_ln_b",
        "L1_ffn_w1", "L1_ffn_b1", "L1_ffn_w2", "L1_ffn_b2"]


def kernel(**inputs):
    import numpy as _np
    import concourse.bacc as _bacc
    from concourse import mybir as _mybir
    from concourse.bass_utils import run_bass_kernel_spmd as _run

    nc = _bacc.Bacc("TRN2", target_bir_lowering=False, num_devices=1)
    arrays, args = {}, []
    for name in _INS + ["rotary"]:
        a = rotary_tables() if name == "rotary" else _np.ascontiguousarray(inputs[name])
        arrays[f"in_{name}_dram"] = a
        args.append(nc.dram_tensor(f"in_{name}_dram", a.shape, _mybir.dt.from_np(a.dtype), kind="ExternalInput").ap())
    args.append(nc.dram_tensor("out_0_dram", (B, T, D), F32, kind="ExternalOutput").ap())
    build(nc, *args)
    r = _run(nc, [arrays], core_ids=[0])
    return r.results[0]["out_0_dram"]
```
